# Optimizing a Trainium2 kernel written in Bass

```python
import numpy as np
import jax
import jax.numpy as jnp

def _softmax(x, axis=-1):
    return jax.nn.softmax(x, axis=axis)

def _gelu(x):
    return jax.nn.gelu(x, approximate=True)

def _silu(x):
    return jax.nn.silu(x)

def _sigmoid(x):
    return jax.nn.sigmoid(x)

def _layernorm(x, axis=-1, eps=1e-05):
    m = jnp.mean(x, axis=axis, keepdims=True)
    v = jnp.var(x, axis=axis, keepdims=True)
    return (x - m) / jnp.sqrt(v + eps)

def _scatter_add(tgt, idx, src, axis=0):
    return tgt.at[idx].add(src)

def _segment_sum(src, seg, n):
    return jax.ops.segment_sum(src, seg, n)
kernel_name = 'mk_decoder_preln_d1_seqx_r2_241b6b'

def setup_inputs(seed: int=0):
    np.random.seed(seed)
    _w = jnp.asarray

    def _rec_inputs():
        import jax
        import jax.numpy as jnp
        _rk = jax.random.key(seed)
        x = -0.0002928 + 1 * jax.random.normal(jax.random.fold_in(_rk, 1), (8, 224, 512), jnp.float32)
        _lenS = 224 - jax.random.randint(jax.random.fold_in(_rk, 7), (8,), 0, max(1, 224 // 4) + 1, jnp.int32)
        _lenS2 = 750 - jax.random.randint(jax.random.fold_in(_rk, 8), (8,), 0, max(1, 750 // 4) + 1, jnp.int32)
        _ctx_1024P = jax.random.normal(jax.random.fold_in(_rk, 11), (8, 16, 512), jnp.float32)
        _ctx_1024c = jax.random.dirichlet(jax.random.fold_in(_rk, 511), 0.3 * jnp.ones((16,), jnp.float32), (8, 750))
        _ctx_1024t = jnp.einsum('bsk,bkd->bsd', _ctx_1024c, _ctx_1024P)
        _ctx_1024t = _ctx_1024t * jax.lax.rsqrt(jnp.mean(jnp.square(_ctx_1024t)) + 1e-12) * 0.953939
        ctx_1024 = -1.39393e-06 + 0.999914 * (_ctx_1024t + 0.3 * jax.random.normal(jax.random.fold_in(_rk, 611), (8, 750, 512), jnp.float32))
        return (x, ctx_1024)
    x, ctx_1024 = _rec_inputs()

    def _L0_attn_setup():
        import jax, jax.numpy as jnp
        import numpy as np
        import math
        N_HEADS = 16
        DIM = 512
        B, S = (2, 1024)

        def _split_heads(x, n_heads):
            b, s, d = x.shape
            dh = d // n_heads
            return x.reshape(b, s, n_heads, dh).transpose(0, 2, 1, 3)
        key = jax.random.key(seed)
        ks = jax.random.split(key, 9)
        std = 0.02
        inp = {'query': jax.random.normal(ks[0], (B, S, DIM), dtype=jnp.float32), 'mask': jnp.ones((B, S), dtype=jnp.int64), 'q_w': jax.random.normal(ks[1], (DIM, DIM), dtype=jnp.float32) * std, 'q_b': jnp.zeros((DIM,), dtype=jnp.float32), 'k_w': jax.random.normal(ks[2], (DIM, DIM), dtype=jnp.float32) * std, 'k_b': jnp.zeros((DIM,), dtype=jnp.float32), 'v_w': jax.random.normal(ks[3], (DIM, DIM), dtype=jnp.float32) * std, 'v_b': jnp.zeros((DIM,), dtype=jnp.float32), 'out_w': jax.random.normal(ks[4], (DIM, DIM), dtype=jnp.float32) * std, 'out_b': jnp.zeros((DIM,), dtype=jnp.float32)}
        return inp
    _L0_attn_all = _L0_attn_setup()
    _L0_attn_in = {k: v for k, v in _L0_attn_all.items() if k in ('mask', 'q_w', 'q_b', 'k_w', 'k_b', 'v_w', 'v_b', 'out_w', 'out_b')}
    del _L0_attn_all

    def _L0_xattn_setup():
        import jax, jax.numpy as jnp
        import numpy as np
        import math
        EMBED = 512
        HEADS = 16
        HEAD_DIM = EMBED // HEADS

        def alibi_slopes(heads: int) -> jnp.ndarray:
            return jnp.asarray([2.0 ** (-8.0 * (h + 1) / heads) for h in range(heads)], dtype=jnp.float32)
        key = jax.random.key(seed)
        ks = jax.random.split(key, 8)
        B, Nq, Nk = (2, 1024, 1024)
        s = 0.02
        return {'query': jax.random.normal(ks[0], (B, Nq, EMBED), jnp.float32), 'kv': jax.random.normal(ks[1], (B, Nk, EMBED), jnp.float32), 'Wq': jax.random.normal(ks[2], (EMBED, EMBED), jnp.float32) * s, 'bq': jnp.zeros((EMBED,), jnp.float32), 'Wkv': jax.random.normal(ks[3], (EMBED, 2 * EMBED), jnp.float32) * s, 'bkv': jnp.zeros((2 * EMBED,), jnp.float32), 'Wo': jax.random.normal(ks[4], (EMBED, EMBED), jnp.float32) * s, 'bo': jnp.zeros((EMBED,), jnp.float32)}
    _L0_xattn_all = _L0_xattn_setup()
    _L0_xattn_in = {k: v for k, v in _L0_xattn_all.items() if k in ('Wq', 'bq', 'Wkv', 'bkv', 'Wo', 'bo')}
    del _L0_xattn_all

    def _L0_ffn_setup():
        import jax, jax.numpy as jnp
        import numpy as np
        D, H, N, K = (512, 1024, 8, 2)
        B, S = (4, 1024)
        key = jax.random.key(seed)
        ks = jax.random.split(key, 4)
        x = jax.random.normal(ks[0], (B, S, D), dtype=jnp.float32)
        Wr = jax.random.normal(ks[1], (N, D), dtype=jnp.float32) / np.sqrt(D)
        br = jnp.zeros((N,), jnp.float32)
        Wl1 = jax.random.normal(ks[2], (N, D, 2 * H), dtype=jnp.float32) / np.sqrt(D)
        bl1 = jnp.zeros((N, 2 * H), jnp.float32)
        Wl2 = jax.random.normal(ks[3], (N, H, D), dtype=jnp.float32) / np.sqrt(H)
        bl2 = jnp.zeros((N, D), jnp.float32)
        biases_N = jnp.zeros((N,), jnp.float32)
        return {'x': x, 'Wr': Wr, 'br': br, 'Wl1': Wl1, 'bl1': bl1, 'Wl2': Wl2, 'bl2': bl2, 'biases_N': biases_N}
    _L0_ffn_all = _L0_ffn_setup()
    _L0_ffn_in = {k: v for k, v in _L0_ffn_all.items() if k in ('Wr', 'br', 'Wl1', 'bl1', 'Wl2', 'bl2', 'biases_N')}
    del _L0_ffn_all
    return {'x': x, 'ctx_1024': ctx_1024, 'L0_attn_mask': _L0_attn_in['mask'], 'L0_attn_q_w': _L0_attn_in['q_w'], 'L0_attn_q_b': _L0_attn_in['q_b'], 'L0_attn_k_w': _L0_attn_in['k_w'], 'L0_attn_k_b': _L0_attn_in['k_b'], 'L0_attn_v_w': _L0_attn_in['v_w'], 'L0_attn_v_b': _L0_attn_in['v_b'], 'L0_attn_out_w': _L0_attn_in['out_w'], 'L0_attn_out_b': _L0_attn_in['out_b'], 'L0_xattn_Wq': _L0_xattn_in['Wq'], 'L0_xattn_bq': _L0_xattn_in['bq'], 'L0_xattn_Wkv': _L0_xattn_in['Wkv'], 'L0_xattn_bkv': _L0_xattn_in['bkv'], 'L0_xattn_Wo': _L0_xattn_in['Wo'], 'L0_xattn_bo': _L0_xattn_in['bo'], 'L0_ffn_Wr': _L0_ffn_in['Wr'], 'L0_ffn_br': _L0_ffn_in['br'], 'L0_ffn_Wl1': _L0_ffn_in['Wl1'], 'L0_ffn_bl1': _L0_ffn_in['bl1'], 'L0_ffn_Wl2': _L0_ffn_in['Wl2'], 'L0_ffn_bl2': _L0_ffn_in['bl2'], 'L0_ffn_biases_N': _L0_ffn_in['biases_N']}

def reference(x, ctx_1024, L0_attn_mask, L0_attn_q_w, L0_attn_q_b, L0_attn_k_w, L0_attn_k_b, L0_attn_v_w, L0_attn_v_b, L0_attn_out_w, L0_attn_out_b, L0_xattn_Wq, L0_xattn_bq, L0_xattn_Wkv, L0_xattn_bkv, L0_xattn_Wo, L0_xattn_bo, L0_ffn_Wr, L0_ffn_br, L0_ffn_Wl1, L0_ffn_bl1, L0_ffn_Wl2, L0_ffn_bl2, L0_ffn_biases_N):
    import jax
    import jax.numpy as jnp

    def _L0_attn_ref(query, mask, q_w, q_b, k_w, k_b, v_w, v_b, out_w, out_b):
        import jax, jax.numpy as jnp
        import numpy as np
        import math
        N_HEADS = 16
        DIM = 512
        B, S = (2, 1024)

        def _split_heads(x, n_heads):
            b, s, d = x.shape
            dh = d // n_heads
            return x.reshape(b, s, n_heads, dh).transpose(0, 2, 1, 3)
        b, s, d = query.shape
        h = N_HEADS
        dh = d // h
        scale = math.sqrt(dh)
        q = _split_heads(query @ q_w.T + q_b, h) / scale
        k = _split_heads(query @ k_w.T + k_b, h)
        v = _split_heads(query @ v_w.T + v_b, h)
        scores = jnp.einsum('bhqd,bhkd->bhqk', q, k)
        attn = jax.nn.softmax(scores.astype(jnp.float32), axis=-1).astype(query.dtype)
        ctx = jnp.einsum('bhqk,bhkd->bhqd', attn, v)
        ctx = ctx.transpose(0, 2, 1, 3).reshape(b, s, d)
        out = ctx @ out_w.T + out_b
        return out

    def _L0_xattn_ref(query, kv, Wq, bq, Wkv, bkv, Wo, bo):
        import jax, jax.numpy as jnp
        import numpy as np
        import math
        EMBED = 512
        HEADS = 16
        HEAD_DIM = EMBED // HEADS

        def alibi_slopes(heads: int) -> jnp.ndarray:
            return jnp.asarray([2.0 ** (-8.0 * (h + 1) / heads) for h in range(heads)], dtype=jnp.float32)
        B, Nq, E = query.shape
        Nk = kv.shape[1]
        H, D = (HEADS, HEAD_DIM)
        q = query @ Wq + bq
        kvp = kv @ Wkv + bkv
        k, v = jnp.split(kvp, 2, axis=-1)
        q = q.reshape(B, Nq, H, D).transpose(0, 2, 1, 3)
        k = k.reshape(B, Nk, H, D).transpose(0, 2, 1, 3)
        v = v.reshape(B, Nk, H, D).transpose(0, 2, 1, 3)
        slopes = alibi_slopes(H)
        rel = jnp.abs(jnp.arange(Nk)[None, :] - jnp.arange(Nq)[:, None] - (Nk - Nq))
        bias = -slopes[:, None, None] * rel.astype(jnp.float32)
        scale = 1.0 / math.sqrt(D)
        scores = jnp.einsum('bhqd,bhkd->bhqk', q, k) * scale + bias[None]
        attn = jax.nn.softmax(scores, axis=-1)
        out = jnp.einsum('bhqk,bhkd->bhqd', attn, v)
        out = out.transpose(0, 2, 1, 3).reshape(B, Nq, E)
        return out @ Wo + bo

    def _L0_ffn_ref(x, Wr, br, Wl1, bl1, Wl2, bl2, biases_N):
        import jax, jax.numpy as jnp
        import numpy as np
        D, H, N, K = (512, 1024, 8, 2)
        B, S = (4, 1024)
        Bb, Ss, Dd = x.shape
        scores_BSN = jnp.einsum('bsd,nd->bsn', x, Wr) + br
        w_BSN = jax.nn.softmax(scores_BSN, axis=-1)
        _, idx_BSK = jax.lax.top_k(scores_BSN + biases_N[None, None, :], K)
        val_BSK = jnp.take_along_axis(w_BSN, idx_BSK, axis=-1)
        val_BSK = val_BSK / jnp.sum(val_BSK, axis=-1, keepdims=True)
        M = Bb * Ss
        x_MD = x.reshape(M, Dd)
        idx_MK = idx_BSK.reshape(M, K)
        val_MK = val_BSK.reshape(M, K)
        h_NM2H = jnp.einsum('md,ndh->nmh', x_MD, Wl1) + bl1[:, None, :]
        a_NMH, b_NMH = (h_NM2H[..., :H], h_NM2H[..., H:])
        y_NMD = jnp.einsum('nmh,nhd->nmd', jax.nn.silu(a_NMH) * b_NMH, Wl2) + bl2[:, None, :]
        ew_MN = jnp.zeros((M, N), x.dtype)
        ew_MN = ew_MN.at[jnp.arange(M)[:, None], idx_MK].set(val_MK)
        y_MD = jnp.einsum('mn,nmd->md', ew_MN, y_NMD)
        return y_MD.reshape(Bb, Ss, Dd)
    x = x + _L0_attn_ref(_layernorm(x, axis=-1), L0_attn_mask, L0_attn_q_w, L0_attn_q_b, L0_attn_k_w, L0_attn_k_b, L0_attn_v_w, L0_attn_v_b, L0_attn_out_w, L0_attn_out_b)
    x = x + _L0_xattn_ref(_layernorm(x, axis=-1), ctx_1024, L0_xattn_Wq, L0_xattn_bq, L0_xattn_Wkv, L0_xattn_bkv, L0_xattn_Wo, L0_xattn_bo)
    x = x + _L0_ffn_ref(_layernorm(x, axis=-1), L0_ffn_Wr, L0_ffn_br, L0_ffn_Wl1, L0_ffn_bl1, L0_ffn_Wl2, L0_ffn_bl2, L0_ffn_biases_N)
    return x

_drawn_inputs = setup_inputs


def setup_inputs(seed=0):
    import zlib

    import numpy as np

    out = dict(_drawn_inputs(seed))
    spreads = {'L0_attn_q_b': (0.0, 0.8),
     'L0_attn_k_b': (0.0, 0.8),
     'L0_attn_v_b': (0.0, 0.1),
     'L0_attn_out_b': (0.0, 0.1),
     'L0_xattn_bq': (0.0, 0.778),
     'L0_xattn_bkv': (0.0, 0.1),
     'L0_xattn_bo': (0.0, 0.1),
     'L0_ffn_br': (0.0, 0.1),
     'L0_ffn_bl1': (0.0, 0.1),
     'L0_ffn_bl2': (0.0, 0.1),
     'L0_ffn_biases_N': (0.0, 0.1)}
    factors = {'L0_attn_q_w': 4.061, 'L0_attn_k_w': 3.798}
    for name, (base, spread) in spreads.items():
        noise = np.random.default_rng([zlib.crc32(name.encode()), seed]).standard_normal(out[name].shape)
        drawn = base * np.exp(spread * noise) if base else spread * noise
        out[name] = jnp.asarray(drawn.astype(out[name].dtype))
    for name, factor in factors.items():
        out[name] = (out[name] * factor).astype(out[name].dtype)
    return out
```

```python
from contextlib import ExitStack

import numpy as np

import concourse.bass as bass
from concourse import mybir

F32 = mybir.dt.float32
F32R = mybir.dt.float32r
I32 = mybir.dt.int32
U32 = mybir.dt.uint32
ALU = mybir.AluOpType
ACT = mybir.ActivationFunctionType
AX = mybir.AxisListType

P = 128
BANK = 512
B, S, D = 8, 224, 512
CTX = 750
KT = D // P
HEADS, DH = 16, 32
GROUPS = HEADS // 4
QR = S // 2
CR = CTX // 6
TOK = B * S
EPS = 1e-5
QSCALE = float(DH) ** -0.5
SHIFT = CTX - S
STEPS = B * GROUPS
DMA = 16


def as_f32(ap):
    return ap.bitcast(F32)


def slope(h):
    return float(np.float32(2.0 ** (-8.0 * (h + 1) / HEADS)))


class Core:

    def __init__(self, nc, sems):
        self.nc = nc
        self.stack = ExitStack()
        self.sems = []

    def __enter__(self):
        self.stack.__enter__()
        return self

    def __exit__(self, *a):
        self.nc.clear_and_free_semaphores(self.sems)
        self.nc.all_engine_barrier()
        return self.stack.__exit__(*a)

    def sb(self, name, shape, dt=F32):
        return self.stack.enter_context(self.nc.sbuf_tensor(name, shape, dt))

    def bank(self, name):
        return self.stack.enter_context(self.nc.psum_tensor(name, [P, BANK], F32))

    def sem(self, name):
        self.sems.append(self.nc.alloc_semaphore(name=name))
        return self.sems[-1]


def linear_phase(nc, sems, tag, *, src, rows, tiles, chunks, ident, weights, stats_ln,
                 transposed, v_out=None, out_proj=None, router=None):
    names = list(weights)
    N = tiles * rows
    n_t = len(transposed)
    out_units = (tiles if out_proj else 0) + 4 * n_t + (tiles if v_out else 0) + (tiles if router else 0)
    OUT = 4
    with Core(nc, sems) as c:
        w_raw = c.sb(f"{tag}_w_raw", [P, KT, D])
        w_hi = {n: c.sb(f"{tag}_{n}_hi", [P, KT, D], F32R) for n in names}
        w_lo = {n: c.sb(f"{tag}_{n}_lo", [P, KT, D], F32R) for n in names}
        x_in = c.sb(f"{tag}_x_in", [rows, 2, tiles, D])
        h = c.sb(f"{tag}_h", [rows, tiles, D]) if stats_ln else None
        hT_hi = c.sb(f"{tag}_hT_hi", [P, KT, N], F32R)
        hT_lo = c.sb(f"{tag}_hT_lo", [P, KT, N], F32R)
        b_col = c.sb(f"{tag}_b_col", [P, max(n_t, 1), KT])
        b_raw = c.sb(f"{tag}_b_raw", [P, max(n_t, 1), KT])
        row_bias = c.sb(f"{tag}_row_bias", [P, 2, D])
        t_hi = c.sb(f"{tag}_t_hi", [P, 2, max(n_t, 1), KT, N], F32R) if n_t else None
        t_lo = c.sb(f"{tag}_t_lo", [P, 2, max(n_t, 1), KT, N], F32R) if n_t else None
        v_sb = c.sb(f"{tag}_v_sb", [rows, 2, tiles, D]) if v_out else None
        if out_proj:
            o_hi = c.sb(f"{tag}_o_hi", [P, KT, N], F32R)
            o_lo = c.sb(f"{tag}_o_lo", [P, KT, N], F32R)
            x_new = c.sb(f"{tag}_x_new", [rows, 2, tiles, D])
        if stats_ln:
            bn = c.sb(f"{tag}_bn", [rows, tiles, 6])
            mv = c.sb(f"{tag}_mv", [rows, tiles, 2])
            veps = c.sb(f"{tag}_veps", [rows, tiles])
            std = c.sb(f"{tag}_std", [rows, tiles])
            rstd = c.sb(f"{tag}_rstd", [rows, tiles])
        if router:
            wr_raw = c.sb(f"{tag}_wr_raw", [8, D])
            wr_T = c.sb(f"{tag}_wr_T", [P, KT, 8])
            hT_f = c.sb(f"{tag}_hT_f", [P, KT, N])
            score = c.sb(f"{tag}_score", [rows, 2, tiles, 8])
        t_bank = [c.bank(f"{tag}_t_bank{i}") for i in range(2)]
        o_bank = [c.bank(f"{tag}_o_bank{i}") for i in range(OUT)]

        w_loaded = [c.sem(f"{tag}_w_loaded_{n}") for n in names]
        bias_loaded = c.sem(f"{tag}_bias_loaded")
        bias_ready = c.sem(f"{tag}_bias_ready")
        x_loaded = [c.sem(f"{tag}_x_loaded{i}") for i in range(2)]
        o_loaded = c.sem(f"{tag}_o_loaded")
        stored = [c.sem(f"{tag}_stored{i}") for i in range(2)]
        t_ready = c.sem(f"{tag}_t_ready")
        hi_ready = c.sem(f"{tag}_hi_ready")
        t_free = c.sem(f"{tag}_t_free")
        out_ready = c.sem(f"{tag}_out_ready")
        ohi_ready = c.sem(f"{tag}_ohi_ready")
        out_free = c.sem(f"{tag}_out_free")
        x_done = c.sem(f"{tag}_x_done")
        bn_done = c.sem(f"{tag}_bn_done")
        bn_seen = c.sem(f"{tag}_bn_seen")
        ag_done = c.sem(f"{tag}_ag_done")
        ve_done = c.sem(f"{tag}_ve_done")
        std_done = c.sem(f"{tag}_std_done")
        rstd_done = c.sem(f"{tag}_rstd_done")
        h_ready = c.sem(f"{tag}_h_ready")
        y_tmp = c.sem(f"{tag}_y_tmp")
        f_ready = c.sem(f"{tag}_f_ready")

        NWU = KT * len(names) + (1 if router else 0)
        n_stores = (tiles if out_proj else 0) * 1 + 2 * 4 * n_t + (tiles if v_out else 0) + \
                   (tiles if router else 0) + (tiles if router else 0)
        n_bias = n_t + (1 if v_out else 0) + (1 if out_proj else 0) + (2 if router else 0)
        lns = tiles if stats_ln else 0

        def rows_of(dram, ch, t):
            return dram[bass.ds((ch * tiles + t) * rows, rows), :]

        block = nc.Block()
        with block as block:
            @block.sync
            def _(sp):
                for i, n in enumerate(names):
                    if i:
                        sp.wait_ge(t_free, KT * i + 2)
                    sp.dma_start(w_raw[:, :, :], weights[n][0].rearrange("(k p) n -> p k n", p=P)).then_inc(w_loaded[i], DMA)
                    if i == 0:
                        for j, (_, bias, _, _) in enumerate(transposed):
                            sp.dma_start(b_raw[:, j, :], bias.rearrange("(m p) -> p m", p=P),
                                         allow_slow_non_contiguous=True).then_inc(bias_loaded, DMA)
                        if v_out:
                            sp.dma_start(row_bias[:, 0, :], v_out[1].partition_broadcast(P)).then_inc(bias_loaded, DMA)
                        if out_proj:
                            sp.dma_start(row_bias[:, 1, :], out_proj[1].partition_broadcast(P)).then_inc(bias_loaded, DMA)
                        if router:
                            sp.dma_start(row_bias[:, 0, 0:8], router[1].partition_broadcast(P)).then_inc(bias_loaded, DMA)
                            sp.dma_start(wr_raw[:, :], router[0]).then_inc(bias_loaded, DMA)
                sp.sem_inc(stored[0], DMA)
                sp.sem_inc(stored[1], DMA)

                def load(ch, i, j):
                    sp.wait_ge(stored[j], DMA + i * (n_stores * DMA))
                    for t in range(tiles):
                        sp.dma_start(x_in[:, j, t, :], rows_of(out_proj[3] if out_proj else src, ch, t)).then_inc(x_loaded[j], DMA)

                def stores(ch, i, j):
                    if out_proj:
                        sp.wait_ge(x_done, (ch + 1) * tiles + 1)
                        for t in range(tiles):
                            sp.dma_start(rows_of(out_proj[4], ch, t), x_new[:, j, t, :]).then_inc(stored[j], DMA)
                    if router:
                        sp.wait_ge(h_ready, (ch + 1) * tiles)
                        for t in range(tiles):
                            sp.dma_start(rows_of(router[3], ch, t), h[:, t, :]).then_inc(stored[j], DMA)
                    base = ch * out_units + (tiles if out_proj else 0) + OUT
                    for q, (_, _, _, dram) in enumerate(transposed):
                        for m in range(KT):
                            sp.wait_ge(out_free, base + q * KT + m + 1)
                            for part, buf in ((0, t_hi), (1, t_lo)):
                                sp.dma_start(dram[part, P * m:P * m + P, bass.ds(ch * N, N)],
                                             as_f32(buf[:, j, q, m, :])).then_inc(stored[j], DMA)
                    if v_out:
                        sp.wait_ge(out_free, base + n_t * KT + tiles)
                        for t in range(tiles):
                            sp.dma_start(rows_of(v_out[2], ch, t), v_sb[:, j, t, :]).then_inc(stored[j], DMA)
                    if router:
                        sp.wait_ge(out_free, base + n_t * KT + tiles)
                        for t in range(tiles):
                            sp.dma_start(rows_of(router[2], ch, t), score[:, j, t, :]).then_inc(stored[j], DMA)

                with sp.Fori(0, chunks // 2) as i:
                    for j in range(2):
                        load(i * 2 + j, i, j)
                        if out_proj:
                            if j == 0:
                                sp.wait_ge(x_done, i * (2 * tiles) + 1)
                            else:
                                sp.wait_ge(x_done, i * (2 * tiles) + tiles + 1)
                            for part, buf in ((0, o_hi), (1, o_lo)):
                                sp.dma_start(as_f32(buf[:, :, :]),
                                             out_proj[2][part].rearrange("(k p) t -> p k t", p=P)[:, :, bass.ds((i * 2 + j) * N, N)]).then_inc(o_loaded, DMA)
                    for j in range(2):
                        stores(i * 2 + j, i, j)
                for j in range(2):
                    sp.wait_ge(stored[j], DMA + (chunks // 2) * n_stores * DMA)

            @block.tensor
            def _(pe):
                for i, n in enumerate(names):
                    if weights[n][1] == "oi":
                        pe.wait_ge(w_loaded[i], DMA)
                        for k in range(KT):
                            u = KT * i + k
                            pe.wait_ge(t_free, u + 1)
                            for o in range(KT):
                                last = pe.transpose(t_bank[u % 2][:, P * o:P * o + P], w_raw[:, o, P * k:P * k + P], ident[:, :])
                            last.then_inc(t_ready, 1)
                    else:
                        if i:
                            pe.wait_ge(t_free, KT * i + 2)
                        pe.sem_inc(t_ready, KT)
                if router:
                    u = KT * len(names)
                    pe.wait_ge(bias_loaded, n_bias * DMA)
                    pe.wait_ge(t_free, u + 1)
                    for k in range(KT):
                        last = pe.transpose(t_bank[u % 2][:, 8 * k:8 * k + 8], wr_raw[:, P * k:P * k + P], ident[0:8, 0:8])
                    last.then_inc(t_ready, 1)

                def products(out, pairs, n):
                    k_n = len(pairs)
                    for q, (a_hi, a_lo, b_hi, b_lo) in enumerate(pairs):
                        pe.matmul(out, a_hi, b_hi, start=(q == 0), stop=False)
                        pe.matmul(out, a_hi, b_lo, start=False, stop=False)
                        last = pe.matmul(out, a_lo, b_hi, start=False, stop=(q == k_n - 1))
                    return last

                def chunk(ch, i, j):
                    unit = 0

                    def slot():
                        return o_bank[(j * out_units + unit) % OUT]

                    if out_proj:
                        pe.wait_ge(o_loaded, (ch + 1) * 2 * DMA)
                        if out_proj:
                            w = out_proj[0]
                        for t in range(tiles):
                            pe.wait_ge(out_free, ch * out_units + unit + 1)
                            cols = slice(rows * t, rows * t + rows)
                            products(slot()[0:rows, :], [(o_hi[:, k, cols], o_lo[:, k, cols], w_hi[w][:, k, :], w_lo[w][:, k, :])
                                                         for k in range(KT)], KT).then_inc(out_ready, 1)
                            unit += 1
                    for k in range(KT):
                        u = NWU + k
                        pe.wait_ge(t_free, ch * KT + NWU + k + 1)
                        for t in range(tiles):
                            if stats_ln:
                                if k == 0:
                                    pe.wait_ge(h_ready, ch * tiles + t + 1)
                                x_t = h[:, t, P * k:P * k + P]
                            else:
                                if k == 0 and t == 0:
                                    pe.wait_ge(x_loaded[j], (i + 1) * (tiles * DMA))
                                x_t = x_in[:, j, t, P * k:P * k + P]
                            last = pe.transpose(t_bank[u % 2][:, rows * t:rows * t + rows], x_t, ident[0:rows, 0:rows])
                        last.then_inc(t_ready, 1)
                    pe.wait_ge(t_free, ch * KT + NWU + KT + 2)
                    for q, (w, _, _, _) in enumerate(transposed):
                        for m in range(KT):
                            pe.wait_ge(out_free, ch * out_units + unit + 1)
                            products(slot()[:, 0:N], [(w_hi[w][:, k, P * m:P * m + P], w_lo[w][:, k, P * m:P * m + P],
                                                       hT_hi[:, k, :], hT_lo[:, k, :]) for k in range(KT)], KT).then_inc(out_ready, 1)
                            unit += 1
                    if v_out:
                        w = v_out[0]
                        for t in range(tiles):
                            pe.wait_ge(out_free, ch * out_units + unit + 1)
                            cols = slice(rows * t, rows * t + rows)
                            products(slot()[0:rows, :], [(hT_hi[:, k, cols], hT_lo[:, k, cols], w_hi[w][:, k, :], w_lo[w][:, k, :])
                                                         for k in range(KT)], KT).then_inc(out_ready, 1)
                            unit += 1
                    if router:
                        for t in range(tiles):
                            pe.wait_ge(out_free, ch * out_units + unit + 1)
                            for k in range(KT):
                                last = pe.matmul(slot()[0:rows, 0:8], hT_f[:, k, rows * t:rows * t + rows], wr_T[:, k, :],
                                                 start=(k == 0), stop=(k == KT - 1))
                            last.then_inc(out_ready, 1)
                            unit += 1

                pe.wait_ge(t_free, NWU + 2)
                with pe.Fori(0, chunks // 2) as i:
                    for j in range(2):
                        chunk(i * 2 + j, i, j)

            @block.scalar
            def _(act):
                for i, n in enumerate(names):
                    act.wait_ge(w_loaded[i], DMA)
                    for k in range(KT):
                        u = KT * i + k
                        act.wait_ge(t_ready, u + 1)
                        raw = t_bank[u % 2][:, :] if weights[n][1] == "oi" else w_raw[:, k, :]
                        act.activation(w_hi[n][:, k, :], raw, ACT.Copy, scale=weights[n][2]).then_inc(hi_ready, 1)
                if router:
                    u = KT * len(names)
                    act.wait_ge(t_ready, u + 1)
                    act.activation(wr_T[:, :, :], t_bank[u % 2][:, 0:8 * KT].rearrange("p (k e) -> p k e", k=KT), ACT.Copy).then_inc(hi_ready, 1)
                act.wait_ge(bias_loaded, n_bias * DMA)
                for q, (_, _, s, _) in enumerate(transposed):
                    act.activation(b_col[:, q, :], b_raw[:, q, :], ACT.Copy, scale=s).then_inc(bias_ready, 1)
                if n_t:
                    act.wait_ge(bias_ready, n_t)

                def chunk(ch, i, j):
                    if stats_ln:
                        act.wait_ge(ve_done, (ch + 1) * 1)
                        act.activation(std[:, :], veps[:, :], ACT.Sqrt).then_inc(std_done, 1)
                    for k in range(KT):
                        act.wait_ge(t_ready, ch * KT + NWU + k + 1)
                        bank = t_bank[(NWU + k) % 2][:, 0:N]
                        if router:
                            act.activation(hT_f[:, k, :], bank, ACT.Copy).then_inc(hi_ready, 1)
                        else:
                            act.activation(hT_hi[:, k, :], bank, ACT.Copy).then_inc(hi_ready, 1)
                    unit = tiles if out_proj else 0
                    if n_t:
                        act.wait_ge(stored[j], DMA + i * (n_stores * DMA))
                    for q in range(n_t):
                        for m in range(KT):
                            act.wait_ge(out_ready, ch * out_units + unit + 1)
                            act.activation(t_hi[:, j, q, m, :], o_bank[(j * out_units + unit) % OUT][:, 0:N], ACT.Identity,
                                           bias=b_col[:, q, m:m + 1]).then_inc(ohi_ready, 1)
                            unit += 1

                with act.Fori(0, chunks // 2) as i:
                    for j in range(2):
                        chunk(i * 2 + j, i, j)

            @block.vector
            def _(dve):
                dve.sem_inc(t_free, 2)
                dve.sem_inc(out_free, OUT)
                if out_proj:
                    dve.sem_inc(x_done, 1)
                for i, n in enumerate(names):
                    for k in range(KT):
                        u = KT * i + k
                        raw = t_bank[u % 2][:, :] if weights[n][1] == "oi" else w_raw[:, k, :]
                        dve.wait_ge(hi_ready, u + 1)
                        dve.scalar_tensor_tensor(w_lo[n][:, k, :], raw, weights[n][2], as_f32(w_hi[n][:, k, :]),
                                                 ALU.mult, ALU.subtract).then_inc(t_free, 1)
                if router:
                    dve.wait_ge(hi_ready, KT * len(names) + 1)
                    dve.sem_inc(t_free, 1)
                dve.wait_ge(bias_loaded, n_bias * DMA)
                if n_t:
                    dve.wait_ge(bias_ready, n_t)

                def chunk(ch, i, j):
                    unit = 0

                    def bank():
                        return o_bank[(j * out_units + unit) % OUT]

                    dve.wait_ge(stored[j], DMA + i * (n_stores * DMA))
                    if out_proj or stats_ln:
                        dve.wait_ge(x_loaded[j], (i + 1) * (tiles * DMA))
                    if out_proj:
                        for t in range(tiles):
                            dve.wait_ge(out_ready, ch * out_units + unit + 1)
                            dve.tensor_tensor(x_new[:, j, t, :], bank()[0:rows, :], row_bias[0:rows, 1, :], ALU.add).then_inc(out_free, 1)
                            dve.wait_ge(out_free, ch * out_units + OUT + unit + 1)
                            dve.tensor_tensor(x_new[:, j, t, :], x_new[:, j, t, :], x_in[:, j, t, :], ALU.add).then_inc(x_done, 1)
                            unit += 1
                    if stats_ln:
                        x = x_new if out_proj else x_in
                        if router:
                            dve.wait_ge(stored[1 - j], DMA + (i + j) * (n_stores * DMA))
                        for t in range(tiles):
                            if out_proj:
                                dve.wait_ge(x_done, ch * tiles + t + 2)
                            dve.bn_stats(bn[:, t, :], x[:, j, t, :]).then_inc(bn_done, 1)
                        dve.wait_ge(bn_done, (ch + 1) * tiles)
                        dve.sem_inc(bn_seen, 1)
                        for t in range(tiles):
                            dve.bn_aggr(mv[:, t, :], bn[:, t, :]).then_inc(ag_done, 1)
                        dve.wait_ge(ag_done, ch * tiles + tiles)
                        dve.tensor_scalar(veps[:, :], mv[:, :, 1], EPS, None, ALU.add).then_inc(ve_done, 1)
                        dve.wait_ge(std_done, ch + 1)
                        dve.reciprocal(rstd[:, :], std[:, :]).then_inc(rstd_done, 1)
                        dve.wait_ge(rstd_done, ch + 1)
                        for t in range(tiles):
                            dve.tensor_scalar(h[:, t, :], x[:, j, t, :], mv[:, t, 0:1], rstd[:, t:t + 1],
                                              ALU.subtract, ALU.mult).then_inc(h_ready, 1)
                    for k in range(KT):
                        dve.wait_ge(hi_ready, ch * KT + NWU + k + 1)
                        if router:
                            dve.sem_inc(t_free, 1)
                        else:
                            dve.tensor_tensor(hT_lo[:, k, :], t_bank[(NWU + k) % 2][:, 0:N], as_f32(hT_hi[:, k, :]), ALU.subtract).then_inc(t_free, 1)
                    for q in range(n_t):
                        for m in range(KT):
                            dve.wait_ge(ohi_ready, ch * (n_t * KT) + q * KT + m + 1)
                            dve.scalar_tensor_tensor(t_lo[:, j, q, m, :], bank()[:, 0:N], b_col[:, q, m:m + 1], as_f32(t_hi[:, j, q, m, :]),
                                                     ALU.add, ALU.subtract).then_inc(out_free, 1)
                            unit += 1
                    if v_out:
                        for t in range(tiles):
                            dve.wait_ge(out_ready, ch * out_units + unit + 1)
                            dve.tensor_tensor(v_sb[:, j, t, :], bank()[0:rows, :], row_bias[0:rows, 0, :], ALU.add).then_inc(out_free, 1)
                            unit += 1
                    if router:
                        for t in range(tiles):
                            dve.wait_ge(out_ready, ch * out_units + unit + 1)
                            dve.tensor_tensor(score[:, j, t, :], bank()[0:rows, 0:8], row_bias[0:rows, 0, 0:8], ALU.add).then_inc(out_free, 1)
                            unit += 1

                with dve.Fori(0, chunks // 2) as i:
                    for j in range(2):
                        chunk(i * 2 + j, i, j)


def constants(nc, sems, ident):
    cleared = sems.enter_context(nc.semaphore("const_cleared"))
    with nc.Block() as block:
        @block.gpsimd
        def _(pool):
            pool.memset(ident[:, :], 0.0).then_inc(cleared, 1)
            pool.wait_ge(cleared, 1)
            pool.affine_select(out=ident[:, :], in_=ident[:, :], compare_op=ALU.not_equal, fill=1.0,
                               base=0, pattern=[[-1, P]], channel_multiplier=1)


def attention_phase(nc, sems, tag, *, qT, kT, v, oT, keys, key_rows, ident, alibi):
    NK = keys // key_rows
    PAIRS = NK // 2
    HALVES = 2 if alibi else 1
    SU = 4 if alibi else 1
    CUTS = (0, 376, 750) if alibi else (0, keys)
    SLOTS = 2
    ROWS = 98
    with Core(nc, sems) as c:
        q_st = c.sb(f"{tag}_q_st", [ROWS, SLOTS, 4, S], F32R)
        k_st = c.sb(f"{tag}_k_st", [ROWS, SLOTS, 4, keys], F32R)
        v_sb = c.sb(f"{tag}_v_sb", [key_rows, SLOTS, NK, P])
        ones = c.sb(f"{tag}_ones", [key_rows, DH])
        prob = c.sb(f"{tag}_prob", [key_rows, 4, NK, S])
        part_max = c.sb(f"{tag}_part_max", [QR, 4, 2, HALVES])
        row_max = c.sb(f"{tag}_row_max", [QR, 2, 4])
        nm_hi = c.sb(f"{tag}_nm_hi", [4, S], F32R)
        nm_lo = c.sb(f"{tag}_nm_lo", [4, S], F32R)
        rinv = c.sb(f"{tag}_rinv", [P, S])
        o_f = c.sb(f"{tag}_o_f", [P, S])
        o_hi = c.sb(f"{tag}_o_hi", [P, S], F32R)
        o_lo = c.sb(f"{tag}_o_lo", [P, S], F32R)
        if alibi:
            rel_q = c.sb(f"{tag}_rel_q", [QR, 2, keys], F32R)
            rel_k = c.sb(f"{tag}_rel_k", [key_rows, NK, S], F32R)
            rel_i = c.sb(f"{tag}_rel_i", [P, NK * S])
            rel_n = c.sb(f"{tag}_rel_n", [P, NK * S])
            d_hi = c.sb(f"{tag}_d_hi", [P, HEADS, P], F32R)
            d_lo = c.sb(f"{tag}_d_lo", [P, HEADS // 2, P], F32R)
        s_bank = [c.bank(f"{tag}_s_bank{i}") for i in range(2)]
        st_bank = [c.bank(f"{tag}_st_bank{i}") for i in range(3 if alibi else 2)]
        m_bank = c.bank(f"{tag}_m_bank")
        o_bank = c.bank(f"{tag}_o_bank")
        r_bank = c.bank(f"{tag}_r_bank")

        const_ready = c.sem(f"{tag}_const_ready")
        const_step = c.sem(f"{tag}_const_step")
        qk_loaded = [c.sem(f"{tag}_qk_loaded{i}") for i in range(SLOTS)]
        v_loaded = [c.sem(f"{tag}_v_loaded{i}") for i in range(SLOTS)]
        s_ready = c.sem(f"{tag}_s_ready")
        s_free = c.sem(f"{tag}_s_free")
        max_ready = c.sem(f"{tag}_max_ready")
        maxT_ready = c.sem(f"{tag}_maxT_ready")
        nmhi_ready = c.sem(f"{tag}_nmhi_ready")
        nm_ready = c.sem(f"{tag}_nm_ready")
        maxrow_loaded = c.sem(f"{tag}_maxrow_loaded")
        st_ready = c.sem(f"{tag}_st_ready")
        exp_done = c.sem(f"{tag}_exp_done")
        pv_done = c.sem(f"{tag}_pv_done")
        rinv_ready = c.sem(f"{tag}_rinv_ready")
        o_ready = c.sem(f"{tag}_o_ready")
        ohi_ready = c.sem(f"{tag}_ohi_ready")
        osplit_ready = c.sem(f"{tag}_osplit_ready")
        o_stored = c.sem(f"{tag}_o_stored")
        o_turn = c.sem(f"{tag}_o_turn")
        store_turn = c.sem(f"{tag}_store_turn")

        STB = len(st_bank)
        SPS, STS = 4 * SU, 4 * PAIRS
        N_CONST = 4 if alibi else 1

        def uses(b, g):
            return b * (GROUPS // SLOTS) + g // SLOTS + 1

        with nc.Block() as block:
            @block.gpsimd
            def _(pool):
                pool.memset(as_f32(k_st[96:98, :, :, :]), 1.0).then_inc(const_step, 1)
                pool.wait_ge(const_step, 1)
                pool.memset(ones[:, :], 1.0).then_inc(const_ready, 1)
                n = 1
                if alibi:
                    grids = [(rel_q[:, t, :], QR, keys, [[1, keys]], -(QR * t + SHIFT), -1) for t in range(2)]
                    grids += [(rel_k[:, :, :].rearrange("p t q -> p (t q)"), key_rows, NK * S, [[key_rows, NK], [-1, S]], -SHIFT, 1)]
                    for out, p, n_cols, pattern, base, mult in grids:
                        plus, minus = rel_i[0:p, 0:n_cols], rel_n[0:p, 0:n_cols]
                        pool.iota(plus, pattern=pattern, base=base, channel_multiplier=mult, allow_small_or_imprecise_dtypes=True).then_inc(const_step, 1)
                        pool.wait_ge(const_step, n + 1)
                        pool.tensor_scalar(minus, plus, -1.0, 0.0, ALU.mult, ALU.max).then_inc(const_step, 1)
                        pool.wait_ge(const_step, n + 2)
                        pool.tensor_scalar(plus, plus, 0.0, None, ALU.max).then_inc(const_step, 1)
                        pool.wait_ge(const_step, n + 3)
                        pool.tensor_tensor(out, minus, plus, ALU.add).then_inc(const_step, 1)
                        pool.wait_ge(const_step, n + 4)
                        n += 4
                    for hd in range(HEADS):
                        pool.tensor_scalar(d_hi[:, hd, :], ident[:, :], -slope(hd), None, ALU.mult).then_inc(const_step, 1)
                        n += 1
                        if hd % 2 == 0:
                            pool.wait_ge(const_step, n)
                            pool.tensor_scalar(rel_i[:, 0:P], ident[:, :], -slope(hd), None, ALU.mult).then_inc(const_step, 1)
                            n += 1
                            pool.wait_ge(const_step, n)
                            pool.tensor_tensor(d_lo[:, hd // 2, :], rel_i[:, 0:P], as_f32(d_hi[:, hd, :]), ALU.subtract).then_inc(const_step, 1)
                            n += 1
                pool.wait_ge(const_step, n)
                pool.sem_inc(const_ready, 1)
                pool.sem_inc(osplit_ready, 1)

                def step(s):
                    pool.wait_ge(o_ready, s + 2)
                    pool.wait_ge(o_stored, (s + 1) * (2 * DMA))
                    pool.sem_inc(o_turn, 1)
                    pool.tensor_copy(o_hi[:, :], o_f[:, :]).then_inc(ohi_ready, 1)
                    pool.wait_ge(ohi_ready, s + 1)
                    pool.tensor_tensor(o_lo[:, :], o_f[:, :], as_f32(o_hi[:, :]), ALU.subtract).then_inc(osplit_ready, 1)

                with pool.Fori(0, B) as b:
                    for g in range(GROUPS):
                        step(b * GROUPS + g)

            @block.sync
            def _(sp):
                def load_qk(b, g):
                    w = g % SLOTS
                    for dst, parts, src, n in ((q_st, (0, 1, 0), qT, S), (k_st, (0, 0, 1), kT, keys)):
                        for r, part in enumerate(parts):
                            sp.dma_start(as_f32(dst[DH * r:DH * r + DH, w, :, :]),
                                         src[part, P * g:P * g + P, bass.ds(b * n, n)].rearrange("(h p) t -> p h t", p=DH)).then_inc(qk_loaded[w], DMA)

                def load_v(b, g):
                    w = g % SLOTS
                    sp.dma_start(v_sb[:, w, :, :],
                                 v[bass.ds(b * keys, keys), P * g:P * g + P].rearrange("(t p) d -> p t d", p=key_rows)).then_inc(v_loaded[w], DMA)

                def step(b, g, last):
                    s = b * GROUPS + g
                    b2, g2 = b + (g + SLOTS) // GROUPS, (g + SLOTS) % GROUPS
                    if not (last and g + SLOTS >= GROUPS):
                        sp.wait_ge(st_ready, (s + 1) * STS)
                        load_qk(b2, g2)
                        sp.wait_ge(pv_done, s + 2)
                        load_v(b2, g2)
                    sp.wait_ge(osplit_ready, s + 2)
                    sp.sem_inc(store_turn, 1)
                    for part, buf in ((0, o_hi), (1, o_lo)):
                        sp.dma_start(oT[part, P * g:P * g + P, bass.ds(b * S, S)], as_f32(buf[:, :])).then_inc(o_stored, DMA)

                sp.sem_inc(o_stored, 2 * DMA)
                for g in range(SLOTS):
                    load_qk(0, g)
                    load_v(0, g)
                with sp.Fori(0, B - 1) as b:
                    for g in range(GROUPS):
                        step(b, g, False)
                for g in range(GROUPS):
                    step(B - 1, g, True)
                sp.wait_ge(o_stored, (STEPS + 1) * 2 * DMA)

            @block.tensor
            def _(pe):
                def first_scores(s, b, g, hh):
                    w = g % SLOTS
                    if hh == 0:
                        pe.wait_ge(qk_loaded[w], uses(b, g) * (6 * DMA))
                    n = 0
                    for half in range(HALVES):
                        for t in range(2):
                            if alibi or t == 0:
                                bank = s_bank[(hh * SU + n) % 2]
                                pe.wait_ge(s_free, s * SPS + hh * SU + n + 1)
                                n += 1
                            col = 0 if alibi else t * keys
                            cols = slice(CUTS[half], CUTS[half + 1])
                            out = bank[0:QR, col:col + cols.stop - cols.start]
                            last = pe.matmul(out, q_st[0:96, w, hh, QR * t:QR * t + QR], k_st[0:96, w, hh, cols], start=True, stop=not alibi)
                            if alibi:
                                last = pe.matmul(out, d_hi[0:QR, 4 * g + hh, 0:QR], rel_q[:, t, cols], start=False, stop=True)
                            if alibi or t == 1:
                                last.then_inc(s_ready, 1)

                def second_scores(s, g, hh):
                    w = g % SLOTS
                    if hh == 0:
                        pe.wait_ge(maxrow_loaded, (s + 2) * (8 * DMA))
                    for u in range(PAIRS):
                        n = hh * PAIRS + u
                        bank = st_bank[(g * STS + n) % STB]
                        pe.wait_ge(exp_done, s * STS + n + 1)
                        for e in range(2):
                            t = 2 * u + e
                            last = pe.matmul(bank[0:key_rows, S * e:S * e + S], k_st[:, w, hh, key_rows * t:key_rows * t + key_rows],
                                             q_st[:, w, hh, :], start=(e == 0), stop=not alibi, skip_group_check=True)
                        if alibi:
                            hd = 4 * g + hh
                            out, r = bank[0:key_rows, 0:2 * S], rel_k[:, 2 * u:2 * u + 2, :]
                            last = pe.matmul(out, d_hi[0:key_rows, hd, 0:key_rows], r, start=False, stop=(hd % 2 == 1), skip_group_check=True)
                            if hd % 2 == 0:
                                last = pe.matmul(out, d_lo[0:key_rows, hd // 2, 0:key_rows], r, start=False, stop=True, skip_group_check=True)
                        last.then_inc(st_ready, 1)

                def transpose_max(s):
                    pe.wait_ge(max_ready, s + 1)
                    pe.wait_ge(nm_ready, s + 1)
                    for t in range(2):
                        last = pe.transpose(m_bank[0:4, QR * t:QR * t + QR], row_max[:, t, :], ident[0:QR, 0:QR])
                    last.then_inc(maxT_ready, 1)

                def values(s, b, g, middle):
                    w = g % SLOTS
                    pe.wait_ge(exp_done, (s + 1) * STS + STB)
                    pe.wait_ge(v_loaded[w], uses(b, g) * DMA)
                    pe.wait_ge(o_ready, s + 1)
                    for bank in (o_bank, r_bank):
                        for t in range(NK):
                            for hh in range(4):
                                a = v_sb[:, w, t, DH * hh:DH * hh + DH] if bank is o_bank else ones[:, :]
                                last = pe.matmul(bank[DH * hh:DH * hh + DH, 0:S], a, prob[:, hh, t, :], start=(t == 0), stop=(t == NK - 1))
                        if bank is o_bank:
                            middle()
                    last.then_inc(pv_done, 1)

                def step(b, g, last):
                    s = b * GROUPS + g
                    ends = last and g == GROUPS - 1
                    b1, g1 = b + (g + 1) // GROUPS, (g + 1) % GROUPS
                    for hh in range(4):
                        second_scores(s, g, hh)
                        if not ends:
                            first_scores(s + 1, b1, g1, hh)
                    values(s, b, g, (lambda: None) if ends else (lambda: transpose_max(s + 1)))

                pe.sem_inc(pv_done, 1)
                pe.sem_inc(maxT_ready, 1)
                pe.wait_ge(const_ready, 2)
                for hh in range(4):
                    first_scores(0, 0, 0, hh)
                transpose_max(0)
                with pe.Fori(0, B - 1) as b:
                    for g in range(GROUPS):
                        step(b, g, False)
                for g in range(GROUPS):
                    step(B - 1, g, True)

            @block.scalar
            def _(act):
                def minus_max(s):
                    act.wait_ge(maxT_ready, s + 2)
                    act.wait_ge(maxrow_loaded, (s + 1) * (8 * DMA))
                    act.activation(nm_hi[:, :], m_bank[0:4, 0:S], ACT.Copy, scale=-1.0).then_inc(nmhi_ready, 1)

                def send_max(s, g):
                    w = g % SLOTS
                    act.wait_ge(nm_ready, s + 2)
                    for r, buf in ((96, nm_hi), (97, nm_lo)):
                        for hh in range(4):
                            act.dma_start(as_f32(q_st[r:r + 1, w, hh, :]), as_f32(buf[hh:hh + 1, :])).then_inc(maxrow_loaded, DMA)

                def step(b, g, last):
                    s = b * GROUPS + g
                    act.wait_ge(pv_done, s + 1)
                    for n in range(STS):
                        act.wait_ge(st_ready, s * STS + n + 1)
                        bank = st_bank[(g * STS + n) % STB]
                        hh, u = n // PAIRS, n % PAIRS
                        act.activation(prob[:, hh, 2 * u:2 * u + 2, :], bank[0:key_rows, 0:2 * S].rearrange("p (e q) -> p e q", e=2),
                                       ACT.Exp).then_inc(exp_done, 1)
                    if not (last and g == GROUPS - 1):
                        minus_max(s + 1)
                        send_max(s + 1, (g + 1) % GROUPS)

                act.sem_inc(exp_done, STB)
                act.sem_inc(maxrow_loaded, 8 * DMA)
                act.wait_ge(const_ready, 2)
                minus_max(0)
                send_max(0, 0)
                with act.Fori(0, B - 1) as b:
                    for g in range(GROUPS):
                        step(b, g, False)
                for g in range(GROUPS):
                    step(B - 1, g, True)

            @block.vector
            def _(dve):
                def maxima(s):
                    for n in range(SPS):
                        dve.wait_ge(s_ready, s * SPS + n + 1)
                        if n == 0 and not alibi:
                            dve.wait_ge(maxT_ready, s + 1)
                        hh = n // SU
                        if alibi:
                            half, t = (n % SU) // 2, n % 2
                            dve.tensor_reduce(part_max[:, hh, t, half:half + 1], s_bank[n % 2][0:QR, 0:CUTS[half + 1] - CUTS[half]], AX.X, ALU.max).then_inc(s_free, 1)
                        else:
                            dve.tensor_reduce(row_max[:, :, hh], s_bank[n % 2][0:QR, 0:2 * keys].rearrange("p (t k) -> p t k", t=2),
                                              AX.X, ALU.max).then_inc(s_free, 1)
                    dve.wait_ge(s_free, (s + 1) * SPS + 2)
                    if alibi:
                        dve.wait_ge(maxT_ready, s + 1)
                        dve.tensor_reduce(row_max[:, :, :].rearrange("p t h -> p h t"), part_max[:, :, :, :], AX.X, ALU.max).then_inc(max_ready, 1)
                    else:
                        dve.sem_inc(max_ready, 1)

                def minus_max_lo(s):
                    dve.wait_ge(nmhi_ready, s + 1)
                    dve.scalar_tensor_tensor(nm_lo[:, :], m_bank[0:4, 0:S], -1.0, as_f32(nm_hi[:, :]), ALU.mult, ALU.subtract).then_inc(nm_ready, 1)

                def normalise(s):
                    dve.wait_ge(pv_done, s + 2)
                    dve.reciprocal(rinv[:, :], r_bank[:, 0:S]).then_inc(rinv_ready, 1)
                    dve.wait_ge(rinv_ready, s + 1)
                    dve.wait_ge(osplit_ready, s + 1)
                    dve.tensor_tensor(o_f[:, :], o_bank[:, 0:S], rinv[:, :], ALU.mult).then_inc(o_ready, 1)

                def step(b, g, last):
                    s = b * GROUPS + g
                    if not (last and g == GROUPS - 1):
                        maxima(s + 1)
                        minus_max_lo(s + 1)
                    normalise(s)

                dve.sem_inc(s_free, 2)
                dve.sem_inc(nm_ready, 1)
                dve.sem_inc(o_ready, 1)
                maxima(0)
                minus_max_lo(0)
                with dve.Fori(0, B - 1) as b:
                    for g in range(GROUPS):
                        step(b, g, False)
                for g in range(GROUPS):
                    step(B - 1, g, True)


EXPERTS, HID = 8, 1024
TILES = TOK // QR
STEP_ROWS = 256
MOE_STEPS = 2 * TOK // STEP_ROWS + EXPERTS
SORTED = (MOE_STEPS + 1) * STEP_ROWS
HCH = 4
HC = HID // HCH


def dispatch_phase(nc, sems, *, score, h, biases, sorted_rows, slot_i, weight, step_expert):
    TE = [QR, TILES, EXPERTS]
    with Core(nc, sems) as c:
        z = c.sb("d_z", TE)
        bias = c.sb("d_bias", [QR, EXPERTS])
        zb = c.sb("d_zb", TE)
        top = c.sb("d_top", TE)
        top_i = c.sb("d_top_i", TE, U32)
        top_f = c.sb("d_top_f", TE)
        iota_e = c.sb("d_iota_e", TE)
        pick = [c.sb(f"d_pick{j}", TE) for j in range(2)]
        mask = c.sb("d_mask", TE)
        before = c.sb("d_before", [QR, TILES + 1, EXPERTS])
        zmax = c.sb("d_zmax", [QR, TILES])
        zs = c.sb("d_zs", TE)
        e = c.sb("d_e", TE)
        esum = c.sb("d_esum", [QR, TILES])
        einv = c.sb("d_einv", [QR, TILES])
        w = c.sb("d_w", TE)
        prod = c.sb("d_prod", TE)
        val = [c.sb(f"d_val{j}", [QR, TILES]) for j in range(2)]
        vsum = c.sb("d_vsum", [QR, TILES])
        vinv = c.sb("d_vinv", [QR, TILES])
        earlier = c.sb("d_earlier", [QR, QR])
        ones = c.sb("d_ones", [QR, P])
        counts_i = c.sb("d_counts_i", [P, EXPERTS], I32)
        n_steps_i = c.sb("d_n_steps_i", [P, EXPERTS], I32)
        n_steps = c.sb("d_n_steps", [P, EXPERTS])
        begin = c.sb("d_begin", [P, EXPERTS + 1])
        first_row = c.sb("d_first_row", [P, EXPERTS])
        row = c.sb("d_row", TE)
        slot_f = c.sb("d_slot_f", [QR, 2, TILES])
        iota_s = c.sb("d_iota_s", [1, MOE_STEPS, EXPERTS])
        past = c.sb("d_past", [1, MOE_STEPS, EXPERTS])
        expert_f = c.sb("d_expert_f", [1, MOE_STEPS])
        h_sb = c.sb("d_h_sb", [QR, TILES, D])
        zeros = c.sb("d_zeros", [P, 2048])
        rank = c.bank("d_rank")
        total = c.bank("d_total")
        loaded, h_loaded = c.sem("d_loaded"), c.sem("d_h_loaded")
        cleared, zeroed = c.sem("d_cleared"), c.sem("d_zeroed")
        consts, consts2 = c.sem("d_consts"), c.sem("d_consts2")
        chain = c.sem("d_chain")
        exp_in, exp_out = c.sem("d_exp_in"), c.sem("d_exp_out")
        mask_ready, rank_ready = c.sem("d_mask_ready"), c.sem("d_rank_ready")
        slot_ready, scattered = c.sem("d_slot_ready"), c.sem("d_scattered")
        per = SORTED * D // P
        n_zero = -(-per // 2048)

        with nc.Block() as block:
            @block.sync
            def _(sp):
                sp.dma_start(z[:, :, :], score.rearrange("(t p) e -> p t e", p=QR)).then_inc(loaded, DMA)
                sp.dma_start(bias[:, :], biases.partition_broadcast(QR)).then_inc(loaded, DMA)
                sp.dma_start(h_sb[:, :, :], h.rearrange("(t p) d -> p t d", p=QR)).then_inc(h_loaded, DMA)
                sp.wait_ge(cleared, 1)
                flat = sorted_rows.rearrange("r d -> (r d)").rearrange("(p n) -> p n", p=P)
                for q in range(n_zero):
                    n = min(2048, per - 2048 * q)
                    sp.dma_start(flat[:, 2048 * q:2048 * q + n], zeros[:, 0:n]).then_inc(zeroed, DMA)

            @block.gpsimd
            def _(pool):
                pool.memset(zeros[:, :], 0.0).then_inc(cleared, 1)
                pool.wait_ge(cleared, 1)
                pool.memset(ones[:, :], 1.0).then_inc(consts, 1)
                pool.wait_ge(consts, 1)
                pool.memset(earlier[:, :], 1.0).then_inc(consts, 1)
                pool.wait_ge(consts, 2)
                pool.affine_select(out=earlier[:, :], in_=earlier[:, :], compare_op=ALU.is_gt, fill=0.0, base=0,
                                   pattern=[[1, QR]], channel_multiplier=-1).then_inc(consts, 1)
                pool.iota(iota_e[:, :, :], pattern=[[0, TILES], [1, EXPERTS]], base=0, channel_multiplier=0,
                          allow_small_or_imprecise_dtypes=True).then_inc(consts, 1)
                pool.iota(iota_s[:, :, :], pattern=[[1, MOE_STEPS], [0, EXPERTS]], base=0, channel_multiplier=0,
                          allow_small_or_imprecise_dtypes=True).then_inc(consts, 1)
                pool.wait_ge(slot_ready, 1)
                pool.wait_ge(h_loaded, DMA)
                pool.wait_ge(zeroed, n_zero * DMA)
                for j in range(2):
                    for t in range(TILES):
                        pool.indirect_dma_start(sorted_rows, bass.IndirectOffsetOnAxis(ap=slot_i[:, j, t:t + 1], axis=0),
                                                h_sb[:, t, :], None).then_inc(scattered, DMA)
                pool.wait_ge(scattered, 2 * TILES * DMA)

            @block.tensor
            def _(pe):
                pe.wait_ge(consts, 5)
                pe.wait_ge(mask_ready, 1)
                te = lambda a: a.rearrange("p t e -> p (t e)")
                pe.matmul(rank[0:QR, 0:P], earlier[:, :], te(mask[:, :, :]), start=True, stop=False)
                pe.matmul(rank[0:QR, 0:P], ones[:, 0:QR], te(before[:, 0:TILES, :]), start=False, stop=True)
                pe.matmul(total[:, 0:EXPERTS], ones[:, :], before[:, TILES, :], start=True, stop=True).then_inc(rank_ready, 1)

            @block.scalar
            def _(act):
                act.wait_ge(exp_in, 1)
                act.activation(e[:, :, :], zs[:, :, :], ACT.Exp).then_inc(exp_out, 1)

            @block.vector
            def _(dve):
                done = [0]

                def then(instruction):
                    done[0] += 1
                    instruction.then_inc(chain, 1)
                    dve.wait_ge(chain, done[0])

                def over_e(a):
                    return a.unsqueeze(2).broadcast_to(TE)

                def over_t(a):
                    return a.unsqueeze(1).broadcast_to(TE)

                dve.wait_ge(loaded, 2 * DMA)
                dve.wait_ge(consts, 5)
                then(dve.tensor_reduce(zmax[:, :], z[:, :, :], AX.X, ALU.max))
                dve.tensor_tensor(zs[:, :, :], z[:, :, :], over_e(zmax[:, :]), ALU.subtract).then_inc(exp_in, 1)
                then(dve.tensor_tensor(zb[:, :, :], z[:, :, :], over_t(bias[:, :]), ALU.add))
                for t in range(TILES):
                    last = dve.max(top[:, t, :], zb[:, t, :])
                then(last)
                for t in range(TILES):
                    last = dve.max_index(top_i[:, t, :], top[:, t, :], zb[:, t, :])
                then(last)
                then(dve.tensor_copy(top_f[:, :, :], top_i[:, :, :]))
                for j in range(2):
                    then(dve.tensor_tensor(pick[j][:, :, :], iota_e[:, :, :], over_e(top_f[:, :, j]), ALU.is_equal))
                then(dve.tensor_tensor(mask[:, :, :], pick[0][:, :, :], pick[1][:, :, :], ALU.add))
                then(dve.memset(before[:, 0, :], 0.0))
                for t in range(TILES):
                    then(dve.tensor_tensor(before[:, t + 1, :], before[:, t, :], mask[:, t, :], ALU.add))
                dve.sem_inc(mask_ready, 1)

                dve.wait_ge(exp_out, 1)
                then(dve.tensor_reduce(esum[:, :], e[:, :, :], AX.X, ALU.add))
                then(dve.reciprocal(einv[:, :], esum[:, :]))
                then(dve.tensor_tensor(w[:, :, :], e[:, :, :], over_e(einv[:, :]), ALU.mult))
                for j in range(2):
                    then(dve.tensor_tensor(prod[:, :, :], w[:, :, :], pick[j][:, :, :], ALU.mult))
                    then(dve.tensor_reduce(val[j][:, :], prod[:, :, :], AX.X, ALU.add))
                then(dve.tensor_tensor(vsum[:, :], val[0][:, :], val[1][:, :], ALU.add))
                then(dve.reciprocal(vinv[:, :], vsum[:, :]))
                for j in range(2):
                    then(dve.tensor_tensor(weight[:, j, :], val[j][:, :], vinv[:, :], ALU.mult))

                dve.wait_ge(rank_ready, 1)
                then(dve.tensor_scalar(counts_i[:, :], total[:, 0:EXPERTS], float(STEP_ROWS - 1), None, ALU.add))
                then(dve.tensor_scalar(n_steps_i[:, :], counts_i[:, :], STEP_ROWS.bit_length() - 1, None, ALU.logical_shift_right))
                then(dve.tensor_copy(n_steps[:, :], n_steps_i[:, :]))
                then(dve.memset(begin[:, 0:1], 0.0))
                for x in range(EXPERTS):
                    then(dve.tensor_tensor(begin[:, x + 1:x + 2], begin[:, x:x + 1], n_steps[:, x:x + 1], ALU.add))
                then(dve.tensor_scalar(first_row[:, :], begin[:, 0:EXPERTS], float(STEP_ROWS), None, ALU.mult))
                then(dve.tensor_tensor(row[:, :, :], rank[0:QR, 0:P].rearrange("p (t e) -> p t e", e=EXPERTS),
                                       over_t(first_row[0:QR, :]), ALU.add))
                for j in range(2):
                    then(dve.tensor_tensor(prod[:, :, :], row[:, :, :], pick[j][:, :, :], ALU.mult))
                    then(dve.tensor_reduce(slot_f[:, j, :], prod[:, :, :], AX.X, ALU.add))
                dve.tensor_copy(slot_i[:, :, :], slot_f[:, :, :]).then_inc(slot_ready, 1)
                SE = [1, MOE_STEPS, EXPERTS]
                then(dve.tensor_tensor(past[:, :, :], iota_s[:, :, :], begin[0:1, 1:EXPERTS + 1].unsqueeze(1).broadcast_to(SE), ALU.is_ge))
                then(dve.tensor_reduce(expert_f[:, :], past[:, :, :], AX.X, ALU.add))
                then(dve.tensor_scalar(step_expert[:, :], expert_f[:, :], float(EXPERTS - 1), None, ALU.min))


def expert_phase(nc, sems, *, sorted_rows, out_rows, w1, b1, w2, b2, step_expert, ident):
    UP = 4
    HT = HC // P
    NU = HCH * HT
    T2 = STEP_ROWS // P
    with Core(nc, sems) as c:
        x_in = c.sb("e_x_in", [P, 2, T2, D])
        xT_hi = c.sb("e_xT_hi", [P, 2, KT, STEP_ROWS], F32R)
        xT_lo = c.sb("e_xT_lo", [P, 2, KT, STEP_ROWS], F32R)
        w1_raw = c.sb("e_w1_raw", [P, HCH, 2, KT, HC])
        w1_hi = c.sb("e_w1_hi", [P, 2, 2, KT, HC], F32R)
        w1_lo = c.sb("e_w1_lo", [P, 2, 2, KT, HC], F32R)
        w2_raw = c.sb("e_w2_raw", [P, HCH, HT, D])
        w2_hi = c.sb("e_w2_hi", [P, 2, HT, D], F32R)
        w2_lo = c.sb("e_w2_lo", [P, 2, HT, D], F32R)
        b1_raw = c.sb("e_b1_raw", [2 * NU, 2, P])
        b1_col = c.sb("e_b1_col", [P, 2, 2 * NU])
        b2_row = c.sb("e_b2_row", [P, 2, D])
        gate = c.sb("e_gate", [P, 2, STEP_ROWS])
        g_f = c.sb("e_g_f", [P, 2, STEP_ROWS])
        g_hi = c.sb("e_g_hi", [P, 4, STEP_ROWS], F32R)
        g_lo = c.sb("e_g_lo", [P, 4, STEP_ROWS], F32R)
        y_sb = c.sb("e_y_sb", [P, 2, T2, D])
        t_bank = [c.bank(f"e_t_bank{i}") for i in range(2)]
        u_bank = [c.bank(f"e_u_bank{i}") for i in range(UP)]
        y_bank = [c.bank(f"e_y_bank{i}") for i in range(T2)]

        x_loaded = [c.sem(f"e_x_loaded{i}") for i in range(2)]
        b_loaded = [c.sem(f"e_b_loaded{i}") for i in range(2)]
        w1_loaded = [c.sem(f"e_w1_loaded{i}") for i in range(HCH)]
        w2_loaded = [c.sem(f"e_w2_loaded{i}") for i in range(HCH)]
        bias_turn = c.sem("e_bias_turn")
        g_turn = c.sem("e_g_turn")
        t_ready = c.sem("e_t_ready")
        xhi_ready = c.sem("e_xhi_ready")
        t_free = c.sem("e_t_free")
        w1hi_ready = c.sem("e_w1hi_ready")
        w1_ready = c.sem("e_w1_ready")
        w2hi_ready = c.sem("e_w2hi_ready")
        w2_ready = c.sem("e_w2_ready")
        up_ready = c.sem("e_up_ready")
        gate_ready = c.sem("e_gate_ready")
        up_free = c.sem("e_up_free")
        ghi_ready = c.sem("e_ghi_ready")
        g_ready = c.sem("e_g_ready")
        down_done = c.sem("e_down_done")
        y_ready = c.sem("e_y_ready")
        y_stored = [c.sem(f"e_y_stored{i}") for i in range(2)]

        def ahead(st, q, n):
            return (st + (q + n) // HCH, (q + n) % HCH)

        def rows_at(dram, step):
            return dram[bass.ds(step * STEP_ROWS, STEP_ROWS), :].rearrange("(t p) d -> p t d", p=P)

        with nc.Block() as block:
            @block.sync
            def _(sp):
                def load_x(step, j, use):
                    sp.wait_ge(t_ready, use)
                    sp.dma_start(x_in[:, j, :, :], rows_at(sorted_rows, step)).then_inc(x_loaded[j], DMA)

                def load_w1(st, q, expert):
                    sp.wait_ge(w1_ready, st * HCH + q + 1)
                    for half in range(2):
                        sp.dma_start(w1_raw[:, q, half, :, :], w1[bass.ds(expert, 1), :, HID * half + HC * q:HID * half + HC * q + HC]
                                     .rearrange("o (k p) n -> p (o k) n", p=P)).then_inc(w1_loaded[q], DMA)

                def load_w2(st, q, expert):
                    sp.wait_ge(w2_ready, st * HCH + q + 1)
                    sp.dma_start(w2_raw[:, q, :, :], w2[bass.ds(expert, 1), HC * q:HC * q + HC, :]
                                 .rearrange("o (t p) d -> p (o t) d", p=P)).then_inc(w2_loaded[q], DMA)

                def step(st, j):
                    expert = sp.value_load(step_expert[0:1, bass.ds(st, 1)], min_val=0, max_val=EXPERTS - 1)
                    sp.wait_ge(t_ready, st * 3 + 1)
                    sp.dma_start(b1_raw[:, j, :], b1[bass.ds(expert, 1), :].rearrange("o (m p) -> (o m) p", p=P)).then_inc(b_loaded[j], DMA)
                    sp.wait_ge(y_ready, st + 1)
                    sp.dma_start(b2_row[:, j, :], b2[bass.ds(expert, 1), :].rearrange("o d -> (o d)").partition_broadcast(P)).then_inc(b_loaded[j], DMA)
                    for q in range(HCH):
                        load_w1(st, q, expert)
                        load_w2(st, q, expert)
                    load_x(st + 1, 1 - j, st * 3 + 1)

                sp.dma_start(x_in[:, 0, :, :], rows_at(sorted_rows, 0)).then_inc(x_loaded[0], DMA)
                with sp.Fori(0, MOE_STEPS // 2) as i:
                    for j in range(2):
                        step(i * 2 + j, j)
                for q in range(2):
                    load_w1(MOE_STEPS, q, EXPERTS - 1)
                load_w2(MOE_STEPS, 0, EXPERTS - 1)
                for j in range(2):
                    sp.wait_ge(y_stored[j], (MOE_STEPS // 2 + 1) * DMA)

            @block.tensor
            def _(pe):
                def turn(st, use, j):
                    pe.wait_ge(x_loaded[j], use * DMA)
                    for q in range(2):
                        pe.wait_ge(t_free, st * 3 + q + 1)
                        for k in range(2):
                            for t in range(T2):
                                last = pe.transpose(t_bank[(j * 3 + q) % 2][:, STEP_ROWS * k + P * t:STEP_ROWS * k + P * t + P],
                                                    x_in[:, j, t, P * (2 * q + k):P * (2 * q + k) + P], ident[:, :])
                        last.then_inc(t_ready, 1)

                def turn_bias(st, i, j):
                    pe.wait_ge(b_loaded[j], (i + 1) * (2 * DMA))
                    pe.wait_ge(t_free, st * 3 + 3)
                    pe.sem_inc(bias_turn, 1)
                    pe.transpose(t_bank[(j * 3 + 2) % 2][:, 0:2 * NU], b1_raw[:, j, :], ident[0:2 * NU, 0:2 * NU]).then_inc(t_ready, 1)

                def up(st, q, j):
                    pe.wait_ge(w1_ready, st * HCH + q + HCH + 1)
                    for t in range(HT):
                        n = q * HT + t
                        pe.wait_ge(up_free, st * NU + n + 1)
                        for half in range(2):
                            out = u_bank[n % UP][:, STEP_ROWS * half:STEP_ROWS * half + STEP_ROWS]
                            for k in range(KT):
                                w_h, w_l = (w[:, q % 2, half, k, P * t:P * t + P] for w in (w1_hi, w1_lo))
                                pe.matmul(out, w_h, xT_hi[:, j, k, :], start=(k == 0), stop=False)
                                pe.matmul(out, w_h, xT_lo[:, j, k, :], start=False, stop=False)
                                last = pe.matmul(out, w_l, xT_hi[:, j, k, :], start=False, stop=(k == KT - 1))
                        last.then_inc(up_ready, 1)

                def down(st, q):
                    pe.wait_ge(w2_ready, st * HCH + q + HCH + 1)
                    pe.wait_ge(g_ready, st * NU + (q + 1) * HT + 2)
                    if q == 0:
                        pe.wait_ge(y_ready, st + 2)
                    for r in range(T2):
                        cols = slice(P * r, P * r + P)
                        for t in range(HT):
                            a_h, a_l = (g[:, (q * HT + t) % 4, cols] for g in (g_hi, g_lo))
                            w_h, w_l = (w[:, q % 2, t, :] for w in (w2_hi, w2_lo))
                            first, end = q == 0 and t == 0, q == HCH - 1 and t == HT - 1
                            pe.matmul(y_bank[r][:, :], a_h, w_h, start=first, stop=False)
                            pe.matmul(y_bank[r][:, :], a_h, w_l, start=False, stop=False)
                            last = pe.matmul(y_bank[r][:, :], a_l, w_h, start=False, stop=end)
                    last.then_inc(down_done, 1)

                def step(st, i, j):
                    turn_bias(st, i, j)
                    pe.wait_ge(t_free, st * 3 + 4)
                    for q in range(HCH):
                        up(st, q, j)
                        if q:
                            down(st, q - 1)
                    turn(st + 1, i + 1 if j == 0 else i + 2, 1 - j)
                    down(st, HCH - 1)

                pe.sem_inc(t_ready, 1)
                pe.sem_inc(up_ready, 2 * HT)
                pe.sem_inc(down_done, 2)
                turn(0, 1, 0)
                with pe.Fori(0, MOE_STEPS // 2) as i:
                    for j in range(2):
                        step(i * 2 + j, i, j)

            @block.scalar
            def _(act):
                def turn(st, j):
                    for q in range(2):
                        act.wait_ge(t_ready, st * 3 + q + 2)
                        act.activation(xT_hi[:, j, 2 * q:2 * q + 2, :], t_bank[(j * 3 + q) % 2][:, :].rearrange("p (k n) -> p k n", k=2),
                                       ACT.Copy).then_inc(xhi_ready, 1)

                def turn_bias(st, j):
                    act.wait_ge(t_ready, st * 3 + 4)
                    act.activation(b1_col[:, j, :], t_bank[(j * 3 + 2) % 2][:, 0:2 * NU], ACT.Copy).then_inc(xhi_ready, 1)
                    act.wait_ge(xhi_ready, st * 3 + 3)

                def split_w1(st, q):
                    act.wait_ge(w1_loaded[q], (st + 1) * (2 * DMA))
                    act.wait_ge(up_ready, (st * HCH + q + 1) * HT)
                    act.activation(w1_hi[:, q % 2, :, :, :], w1_raw[:, q, :, :, :], ACT.Copy).then_inc(w1hi_ready, 1)

                def split_w2(st, q):
                    act.wait_ge(w2_loaded[q], (st + 1) * DMA)
                    act.wait_ge(down_done, st * HCH + q + 1)
                    act.activation(w2_hi[:, q % 2, :, :], w2_raw[:, q, :, :], ACT.Copy).then_inc(w2hi_ready, 1)

                def gates(st, q, j):
                    for t in range(HT):
                        n = q * HT + t
                        act.wait_ge(up_ready, st * NU + n + 2 * HT + 1)
                        act.wait_ge(up_free, st * NU + n + UP - 1)
                        act.activation(gate[:, n % 2, :], u_bank[n % UP][:, 0:STEP_ROWS], ACT.Silu,
                                       bias=b1_col[:, j, n:n + 1]).then_inc(gate_ready, 1)

                def step(st, j):
                    turn_bias(st, j)
                    for q in range(HCH):
                        gates(st, q, j)
                        if q == HCH - 1:
                            turn(st + 1, 1 - j)
                        split_w2(*ahead(st, q, 1))
                        split_w1(*ahead(st, q, 2))
                    act.wait_ge(y_ready, st + 3)
                    act.dma_start(rows_at(out_rows, st), y_sb[:, j, :, :]).then_inc(y_stored[j], DMA)

                act.sem_inc(y_stored[0], DMA)
                act.sem_inc(y_stored[1], DMA)
                turn(0, 0)
                split_w1(0, 0)
                split_w1(0, 1)
                split_w2(0, 0)
                with act.Fori(0, MOE_STEPS // 2) as i:
                    for j in range(2):
                        step(i * 2 + j, j)

            @block.gpsimd
            def _(pool):
                def split_w2(st, q):
                    pool.wait_ge(w2hi_ready, st * HCH + q + 1)
                    pool.tensor_tensor(w2_lo[:, q % 2, :, :], w2_raw[:, q, :, :], as_f32(w2_hi[:, q % 2, :, :]),
                                       ALU.subtract).then_inc(w2_ready, 1)

                def split_gated(st, q):
                    pool.wait_ge(down_done, st * HCH + q + 1)
                    for t in range(HT):
                        n = q * HT + t
                        pool.wait_ge(up_free, st * NU + n + UP + 1)
                        pool.sem_inc(g_turn, 1)
                        pool.tensor_copy(g_hi[:, n % 4, :], g_f[:, n % 2, :]).then_inc(ghi_ready, 1)
                        pool.wait_ge(ghi_ready, st * NU + n + 1)
                        pool.tensor_tensor(g_lo[:, n % 4, :], g_f[:, n % 2, :], as_f32(g_hi[:, n % 4, :]),
                                           ALU.subtract).then_inc(g_ready, 1)

                def step(st, j):
                    for q in range(HCH):
                        split_gated(st, q)
                        split_w2(*ahead(st, q, 1))

                pool.sem_inc(w2_ready, HCH)
                pool.sem_inc(g_ready, 2)
                split_w2(0, 0)
                with pool.Fori(0, MOE_STEPS // 2) as i:
                    for j in range(2):
                        step(i * 2 + j, j)

            @block.vector
            def _(dve):
                def turn(st, j):
                    for q in range(2):
                        dve.wait_ge(xhi_ready, st * 3 + q + 1)
                        dve.tensor_tensor(xT_lo[:, j, 2 * q:2 * q + 2, :], t_bank[(j * 3 + q) % 2][:, :].rearrange("p (k n) -> p k n", k=2),
                                          as_f32(xT_hi[:, j, 2 * q:2 * q + 2, :]), ALU.subtract).then_inc(t_free, 1)

                def split_w1(st, q):
                    dve.wait_ge(w1hi_ready, st * HCH + q + 1)
                    dve.tensor_tensor(w1_lo[:, q % 2, :, :, :], w1_raw[:, q, :, :, :], as_f32(w1_hi[:, q % 2, :, :, :]),
                                      ALU.subtract).then_inc(w1_ready, 1)

                def gated(st, q, j):
                    for t in range(HT):
                        n = q * HT + t
                        dve.wait_ge(gate_ready, st * NU + n + 1)
                        dve.wait_ge(g_ready, st * NU + n + 1)
                        dve.scalar_tensor_tensor(g_f[:, n % 2, :], u_bank[n % UP][:, STEP_ROWS:2 * STEP_ROWS],
                                                 b1_col[:, j, NU + n:NU + n + 1], gate[:, n % 2, :],
                                                 ALU.add, ALU.mult).then_inc(up_free, 1)

                def step(st, i, j):
                    dve.wait_ge(xhi_ready, st * 3 + 3)
                    dve.wait_ge(t_free, st * 3 + 4)
                    dve.sem_inc(t_free, 1)
                    for q in range(HCH):
                        gated(st, q, j)
                        if q == HCH - 1:
                            turn(st + 1, 1 - j)
                        split_w1(*ahead(st, q, 2))
                    dve.wait_ge(down_done, (st + 1) * HCH + 2)
                    dve.wait_ge(b_loaded[j], (i + 1) * (2 * DMA))
                    dve.wait_ge(y_stored[j], (i + 1) * DMA)
                    for r in range(T2):
                        last = dve.tensor_tensor(y_sb[:, j, r, :], y_bank[r][:, :], b2_row[:, j, :], ALU.add)
                    last.then_inc(y_ready, 1)

                dve.sem_inc(t_free, 2)
                dve.sem_inc(w1_ready, HCH)
                dve.sem_inc(up_free, UP)
                dve.sem_inc(y_ready, 2)
                turn(0, 0)
                split_w1(0, 0)
                split_w1(0, 1)
                with dve.Fori(0, MOE_STEPS // 2) as i:
                    for j in range(2):
                        step(i * 2 + j, i, j)


def combine_phase(nc, sems, *, x, out_rows, slot_i, weight, out):
    with Core(nc, sems) as c:
        x_sb = c.sb("c_x", [QR, TILES, D])
        y = [c.sb(f"c_y{j}", [QR, TILES, D]) for j in range(2)]
        x_loaded = c.sem("c_x_loaded")
        gathered = [c.sem(f"c_gathered{t}") for t in range(TILES)]
        added = [c.sem(f"c_added{j}") for j in range(2)]
        stored = c.sem("c_stored")
        tiles = "(t p) d -> p t d"
        with nc.Block() as block:
            @block.sync
            def _(sp):
                sp.dma_start(x_sb[:, :, :], x.rearrange(tiles, p=QR)).then_inc(x_loaded, DMA)
                for t in range(0, TILES, 2):
                    sp.wait_ge(added[1], t + 2)
                    sp.dma_start(out.rearrange(tiles, p=QR)[:, t:t + 2, :], x_sb[:, t:t + 2, :]).then_inc(stored, DMA)
                sp.wait_ge(stored, TILES // 2 * DMA)

            @block.gpsimd
            def _(pool):
                for t in range(TILES):
                    for j in range(2):
                        pool.indirect_dma_start(y[j][:, t, :], None, out_rows,
                                                bass.IndirectOffsetOnAxis(ap=slot_i[:, j, t:t + 1], axis=0)).then_inc(gathered[t], DMA)

            @block.vector
            def _(dve):
                dve.wait_ge(x_loaded, DMA)
                for t in range(TILES):
                    dve.wait_ge(gathered[t], 2 * DMA)
                    for j in range(2):
                        if j:
                            dve.wait_ge(added[0], t + 1)
                        dve.scalar_tensor_tensor(x_sb[:, t, :], y[j][:, t, :], weight[:, j, t:t + 1], x_sb[:, t, :],
                                                 ALU.mult, ALU.add).then_inc(added[j], 1)


INPUTS = ["x", "ctx_1024"] + ["L0_attn_" + n for n in ("q_w", "q_b", "k_w", "k_b", "v_w", "v_b", "out_w", "out_b")] + \
         ["L0_xattn_" + n for n in ("Wq", "bq", "Wkv", "bkv", "Wo", "bo")] + \
         ["L0_ffn_" + n for n in ("Wr", "br", "Wl1", "bl1", "Wl2", "bl2", "biases_N")]


def build(nc, d, out):
    def scratch(name, shape):
        return nc.dram_tensor(name, shape, F32, kind="Internal").ap()

    flat = "b s d -> (b s) d"
    x, ctx = d["x"].rearrange(flat), d["ctx_1024"].rearrange(flat)
    qT1, kT1, oT1, qT2, oT2 = (scratch(n, [2, D, TOK]) for n in ("qT1", "kT1", "oT1", "qT2", "oT2"))
    kT2, v2 = scratch("kT2", [2, D, B * CTX]), scratch("v2", [B * CTX, D])
    v1, x1, x2, h = (scratch(n, [TOK, D]) for n in ("v1", "x1", "x2", "h_moe"))
    score = scratch("score", [TOK, EXPERTS])
    sorted_rows, out_rows = scratch("sorted_rows", [SORTED, D]), scratch("out_rows", [MOE_STEPS * STEP_ROWS, D])
    a, c, f = "L0_attn_", "L0_xattn_", "L0_ffn_"
    token_tiles = dict(rows=QR, tiles=4, chunks=TOK // QR // 4)

    with ExitStack() as sems:
        ident = sems.enter_context(nc.sbuf_tensor("ident", [P, P], F32))
        slot_i = sems.enter_context(nc.sbuf_tensor("slot_i", [QR, 2, TILES], U32))
        weight = sems.enter_context(nc.sbuf_tensor("weight", [QR, 2, TILES], F32))
        step_expert = sems.enter_context(nc.sbuf_tensor("step_expert", [1, MOE_STEPS], I32))
        constants(nc, sems, ident)
        linear_phase(nc, sems, "p1", src=x, ident=ident, **token_tiles, stats_ln=True,
                     weights={"wq": (d[a + "q_w"], "oi", QSCALE), "wk": (d[a + "k_w"], "oi", 1.0), "wv": (d[a + "v_w"], "oi", 1.0)},
                     transposed=[("wq", d[a + "q_b"], QSCALE, qT1), ("wk", d[a + "k_b"], 1.0, kT1)],
                     v_out=("wv", d[a + "v_b"], v1))
        linear_phase(nc, sems, "p2", src=ctx, ident=ident, rows=CR, tiles=4, chunks=B * CTX // CR // 4, stats_ln=False,
                     weights={"wk": (d[c + "Wkv"][:, 0:D], "io", 1.0), "wv": (d[c + "Wkv"][:, D:2 * D], "io", 1.0)},
                     transposed=[("wk", d[c + "bkv"][0:D], 1.0, kT2)], v_out=("wv", d[c + "bkv"][D:2 * D], v2))
        attention_phase(nc, sems, "a1", qT=qT1, kT=kT1, v=v1, oT=oT1, keys=S, key_rows=QR, ident=ident, alibi=False)
        linear_phase(nc, sems, "o1", src=None, ident=ident, **token_tiles, stats_ln=True,
                     weights={"wo": (d[a + "out_w"], "oi", 1.0), "wq": (d[c + "Wq"], "io", QSCALE)},
                     out_proj=("wo", d[a + "out_b"], oT1, x, x1),
                     transposed=[("wq", d[c + "bq"], QSCALE, qT2)])
        attention_phase(nc, sems, "a2", qT=qT2, kT=kT2, v=v2, oT=oT2, keys=CTX, key_rows=CR, ident=ident, alibi=True)
        linear_phase(nc, sems, "o2", src=None, ident=ident, **token_tiles, stats_ln=True,
                     weights={"wo": (d[c + "Wo"], "io", 1.0)},
                     out_proj=("wo", d[c + "bo"], oT2, x1, x2), transposed=[],
                     router=(d[f + "Wr"], d[f + "br"], score, h))
        dispatch_phase(nc, sems, score=score, h=h, biases=d[f + "biases_N"], sorted_rows=sorted_rows,
                       slot_i=slot_i, weight=weight, step_expert=step_expert)
        expert_phase(nc, sems, sorted_rows=sorted_rows, out_rows=out_rows, w1=d[f + "Wl1"], b1=d[f + "bl1"],
                     w2=d[f + "Wl2"], b2=d[f + "bl2"], step_expert=step_expert, ident=ident)
        combine_phase(nc, sems, x=x2, out_rows=out_rows, slot_i=slot_i, weight=weight, out=out.rearrange(flat))


def kernel(**inputs):
    import concourse.bacc as bacc
    from concourse.bass_utils import run_bass_kernel_spmd

    nc = bacc.Bacc("TRN2", target_bir_lowering=False, num_devices=1)
    arrays = {n: np.ascontiguousarray(inputs[n]) for n in INPUTS}
    d = {n: nc.dram_tensor(n, a.shape, F32, kind="ExternalInput").ap() for n, a in arrays.items()}
    out = nc.dram_tensor("out", (B, S, D), F32, kind="ExternalOutput").ap()
    build(nc, d, out)
    return run_bass_kernel_spmd(nc, [arrays], core_ids=[0]).results[0]["out"]
```

```python
from contextlib import ExitStack

import numpy as np

import concourse.bass as bass
from concourse import mybir

F32 = mybir.dt.float32
F32R = mybir.dt.float32r
I32 = mybir.dt.int32
U32 = mybir.dt.uint32
ALU = mybir.AluOpType
ACT = mybir.ActivationFunctionType
AX = mybir.AxisListType

P = 128
BANK = 512
B, S, D = 8, 224, 512
CTX = 750
KT = D // P
HEADS, DH = 16, 32
GROUPS = HEADS // 4
QR = S // 2
CR = CTX // 6
TOK = B * S
EPS = 1e-5
QSCALE = float(DH) ** -0.5
SHIFT = CTX - S
STEPS = B * GROUPS
DMA = 16
QUERY_PARTS, KEY_PARTS = (0, 1, 0), (0, 0, 1)


def as_f32(ap):
    return ap.bitcast(F32)


def slope(h):
    return float(np.float32(2.0 ** (-8.0 * (h + 1) / HEADS)))


class Core:

    def __init__(self, nc, sems):
        self.nc = nc
        self.stack = ExitStack()
        self.sems = []

    def __enter__(self):
        self.stack.__enter__()
        return self

    def __exit__(self, *a):
        self.nc.clear_and_free_semaphores(self.sems)
        self.nc.all_engine_barrier()
        return self.stack.__exit__(*a)

    def sb(self, name, shape, dt=F32):
        return self.stack.enter_context(self.nc.sbuf_tensor(name, shape, dt))

    def bank(self, name):
        return self.stack.enter_context(self.nc.psum_tensor(name, [P, BANK], F32))

    def sem(self, name):
        self.sems.append(self.nc.alloc_semaphore(name=name))
        return self.sems[-1]


def linear_phase(nc, sems, tag, *, src, rows, tiles, chunks, ident, weights, stats_ln,
                 transposed, v_out=None, out_proj=None, router=None):
    names = list(weights)
    N = tiles * rows
    n_t = len(transposed)
    n_first = tiles if out_proj else 0
    out_units = n_first + KT * n_t + (tiles if v_out else 0) + (tiles if router else 0)
    OUT = 4
    assert out_units % OUT == 0 and n_first % OUT == 0 and chunks % 2 == 0
    by_row = "(t p) d -> p t d"
    with Core(nc, sems) as c:
        w_raw = c.sb(f"{tag}_w_raw", [P, 2, KT, D])
        w_hi = {n: c.sb(f"{tag}_{n}_hi", [P, KT, D], F32R) for n in names}
        w_lo = {n: c.sb(f"{tag}_{n}_lo", [P, KT, D], F32R) for n in names}
        x_in = c.sb(f"{tag}_x_in", [rows, 2, tiles, D])
        h = c.sb(f"{tag}_h", [rows, tiles, D]) if stats_ln else None
        hT_hi = c.sb(f"{tag}_hT_hi", [P, 2, KT, N], F32R) if not router else None
        hT_lo = c.sb(f"{tag}_hT_lo", [P, 2, KT, N], F32R) if not router else None
        if n_t:
            b_raw = c.sb(f"{tag}_b_raw", [P, n_t, KT])
            b_col = c.sb(f"{tag}_b_col", [P, n_t, KT])
            t_hi = c.sb(f"{tag}_t_hi", [P, 2, n_t, KT, N], F32R)
            t_lo = c.sb(f"{tag}_t_lo", [P, 2, n_t, KT, N], F32R)
        if v_out:
            v_bias = c.sb(f"{tag}_v_bias", [P, D])
            v_sb = c.sb(f"{tag}_v_sb", [rows, 2, tiles, D])
        if out_proj:
            out_bias = c.sb(f"{tag}_out_bias", [P, D])
            o_split = c.sb(f"{tag}_o_split", [P, 2, 2, KT, N], F32R)
            x_new = c.sb(f"{tag}_x_new", [rows, 2, tiles, D])
        if stats_ln:
            bn = c.sb(f"{tag}_bn", [rows, tiles, 6])
            mv = c.sb(f"{tag}_mv", [rows, tiles, 2])
            veps = c.sb(f"{tag}_veps", [rows, tiles])
            std = c.sb(f"{tag}_std", [rows, tiles])
            rstd = c.sb(f"{tag}_rstd", [rows, tiles])
        if router:
            r_bias = c.sb(f"{tag}_r_bias", [P, 8])
            wr_raw = c.sb(f"{tag}_wr_raw", [8, D])
            wr_T = c.sb(f"{tag}_wr_T", [P, KT, 8])
            hT_f = c.sb(f"{tag}_hT_f", [P, 2, KT, N])
            score = c.sb(f"{tag}_score", [rows, 2, tiles, 8])
        t_bank = [c.bank(f"{tag}_t_bank{i}") for i in range(2)]
        o_bank = [c.bank(f"{tag}_o_bank{i}") for i in range(OUT)]

        w_loaded = [c.sem(f"{tag}_w_loaded_{n}") for n in names]
        bias_loaded = c.sem(f"{tag}_bias_loaded")
        bias_ready = c.sem(f"{tag}_bias_ready")
        x_loaded = [c.sem(f"{tag}_x_loaded{i}") for i in range(2)]
        o_loaded = [c.sem(f"{tag}_o_loaded{i}") for i in range(2)]
        x_stored = [c.sem(f"{tag}_x_stored{i}") for i in range(2)]
        h_stored = c.sem(f"{tag}_h_stored")
        stored = [c.sem(f"{tag}_stored{i}") for i in range(2)]
        t_ready = c.sem(f"{tag}_t_ready")
        hi_ready = c.sem(f"{tag}_hi_ready")
        t_free = c.sem(f"{tag}_t_free")
        out_ready = c.sem(f"{tag}_out_ready")
        ohi_ready = c.sem(f"{tag}_ohi_ready")
        out_free = c.sem(f"{tag}_out_free")
        x_done = c.sem(f"{tag}_x_done")
        bn_done = c.sem(f"{tag}_bn_done")
        bn_seen = c.sem(f"{tag}_bn_seen")
        ag_done = c.sem(f"{tag}_ag_done")
        ve_done = c.sem(f"{tag}_ve_done")
        std_done = c.sem(f"{tag}_std_done")
        rstd_done = c.sem(f"{tag}_rstd_done")
        h_ready = c.sem(f"{tag}_h_ready")
        load_turn = c.sem(f"{tag}_load_turn")

        NWU = KT * len(names) + (1 if router else 0)
        n_stores = 3 * KT * n_t + (1 if v_out else 0) + (1 if router else 0)
        n_bias = n_t + (1 if v_out else 0) + (1 if out_proj else 0) + (2 if router else 0)
        AHEAD = 2 * tiles

        def rows_of(dram, ch):
            return dram[bass.ds(ch * N, N), :].rearrange(by_row, p=rows)

        def run(step):
            def body(engine):
                with engine.Fori(0, chunks // 2 - 1) as i:
                    for j in range(2):
                        step(i * 2 + j, i, j, True)
                for j in range(2):
                    step(chunks - 2 + j, chunks // 2 - 1, j, j == 0)
            return body

        def following(i, j):
            return (i, 1) if j == 0 else (i + 1, 0)

        def unit(ch, k):
            return ch * out_units + n_first + k

        with nc.Block() as block:
            @block.gpsimd
            def _(pool):
                def load(ch, j):
                    if out_proj:
                        pool.wait_ge(x_done, (ch + 1) * tiles)
                    elif stats_ln:
                        pool.wait_ge(h_ready, (ch + 1) * tiles)
                    else:
                        pool.wait_ge(t_ready, ch * KT + NWU - KT)
                    pool.sem_inc(load_turn, 1)
                    pool.dma_start(x_in[:, j, :, :], rows_of(out_proj[3] if out_proj else src, ch)).then_inc(x_loaded[j], DMA)
                    if out_proj:
                        for part in range(2):
                            pool.dma_start(as_f32(o_split[:, j, part, :, :]),
                                           out_proj[2][part].rearrange("(k p) t -> p k t", p=P)[:, :, bass.ds(ch * N, N)]).then_inc(o_loaded[j], DMA)

                with pool.Fori(0, chunks // 2) as i:
                    for j in range(2):
                        load(i * 2 + j, j)

            @block.sync
            def _(sp):
                for i, n in enumerate(names):
                    if i >= 2:
                        sp.wait_ge(t_free, KT * (i - 1) + 2)
                    sp.dma_start(w_raw[:, i % 2, :, :], weights[n][0].rearrange("(k p) n -> p k n", p=P)).then_inc(w_loaded[i], DMA)
                    if i == 0:
                        for j, (_, bias, _, _, _) in enumerate(transposed):
                            sp.dma_start(b_raw[:, j, :], bias.rearrange("(m p) -> p m", p=P),
                                         allow_slow_non_contiguous=True).then_inc(bias_loaded, DMA)
                        if v_out:
                            sp.dma_start(v_bias[:, :], v_out[1].partition_broadcast(P)).then_inc(bias_loaded, DMA)
                        if out_proj:
                            sp.dma_start(out_bias[:, :], out_proj[1].partition_broadcast(P)).then_inc(bias_loaded, DMA)
                        if router:
                            sp.dma_start(r_bias[:, :], router[1].partition_broadcast(P)).then_inc(bias_loaded, DMA)
                            sp.dma_start(wr_raw[:, :], router[0]).then_inc(bias_loaded, DMA)
                for j in range(2):
                    sp.sem_inc(stored[j], DMA)
                    sp.sem_inc(x_stored[j], DMA)
                sp.sem_inc(h_stored, DMA)

                def store_rows(ch, j):
                    if out_proj:
                        sp.wait_ge(x_done, (ch + 1) * tiles + AHEAD)
                        sp.sem_inc(load_turn, 1)
                        sp.dma_start(rows_of(out_proj[4], ch), x_new[:, j, :, :]).then_inc(x_stored[j], DMA)
                    if router:
                        sp.wait_ge(h_ready, (ch + 1) * tiles + AHEAD)
                        sp.sem_inc(load_turn, 1)
                        sp.dma_start(rows_of(router[3], ch), h[:, :, :]).then_inc(h_stored, DMA)

                def step(ch, i, j, more):
                    if more:
                        store_rows(ch + 1, 1 - j)
                    k = n_first if more else 0
                    for q, (_, _, _, dram, parts) in enumerate(transposed):
                        for m in range(KT):
                            k += 1
                            sp.wait_ge(out_free, unit(ch, k) + OUT)
                            sp.sem_inc(load_turn, 1)
                            for r, part in enumerate(parts):
                                sp.dma_start(dram[m, DH * r:DH * r + DH, :, bass.ds(ch * N, N)].rearrange("p h t -> h p t"),
                                             as_f32((t_hi, t_lo)[part][:, j, q, m, :])).then_inc(stored[j], DMA)
                    for out, dram in ((v_out and v_sb, v_out and v_out[2]), (router and score, router and router[2])):
                        if out:
                            k += tiles
                            sp.wait_ge(out_free, unit(ch, k) + OUT)
                            sp.sem_inc(load_turn, 1)
                            sp.dma_start(rows_of(dram, ch), out[:, j, :, :]).then_inc(stored[j], DMA)

                store_rows(0, 0)
                run(step)(sp)
                for j in range(2):
                    sp.wait_ge(stored[j], DMA + chunks // 2 * n_stores * DMA)
                    if out_proj:
                        sp.wait_ge(x_stored[j], DMA + chunks // 2 * DMA)
                if router:
                    sp.wait_ge(h_stored, DMA + chunks * DMA)

            @block.tensor
            def _(pe):
                for i, n in enumerate(names):
                    if weights[n][1] == "oi":
                        pe.wait_ge(w_loaded[i], DMA)
                        for k in range(KT):
                            u = KT * i + k
                            pe.wait_ge(t_free, u + 1)
                            for o in range(KT):
                                last = pe.transpose(t_bank[u % 2][:, P * o:P * o + P], w_raw[:, i % 2, o, P * k:P * k + P], ident[:, :])
                            last.then_inc(t_ready, 1)
                    else:
                        if i:
                            pe.wait_ge(t_free, KT * i + 2)
                        pe.sem_inc(t_ready, KT)
                if router:
                    u = KT * len(names)
                    pe.wait_ge(bias_loaded, n_bias * DMA)
                    pe.wait_ge(t_free, u + 1)
                    for k in range(KT):
                        last = pe.transpose(t_bank[u % 2][:, 8 * k:8 * k + 8], wr_raw[:, P * k:P * k + P], ident[0:8, 0:8])
                    last.then_inc(t_ready, 1)

                def products(out, pairs):
                    for q, (a_hi, a_lo, b_hi, b_lo) in enumerate(pairs):
                        pe.matmul(out, a_hi, b_hi, start=(q == 0), stop=False)
                        pe.matmul(out, a_hi, b_lo, start=False, stop=False)
                        last = pe.matmul(out, a_lo, b_hi, start=False, stop=(q == len(pairs) - 1))
                    return last

                def project_out(ch, i, j, u, k):
                    w = out_proj[0]
                    pe.wait_ge(o_loaded[j], (i + 1) * (2 * DMA))
                    for t in range(tiles):
                        pe.wait_ge(out_free, u + k + t + 1)
                        cols = slice(rows * t, rows * t + rows)
                        products(o_bank[(k + t) % OUT][0:rows, :],
                                 [(o_split[:, j, 0, q, cols], o_split[:, j, 1, q, cols], w_hi[w][:, q, :], w_lo[w][:, q, :])
                                  for q in range(KT)]).then_inc(out_ready, 1)

                def turn(ch, i, j):
                    for k in range(KT):
                        pe.wait_ge(t_free, ch * KT + NWU + k + 1)
                        for t in range(tiles):
                            if stats_ln:
                                if k == 0:
                                    pe.wait_ge(h_ready, ch * tiles + t + 1 + AHEAD)
                                x_t = h[:, t, P * k:P * k + P]
                            else:
                                if k == 0 and t == 0:
                                    pe.wait_ge(x_loaded[j], (i + 1) * DMA)
                                x_t = x_in[:, j, t, P * k:P * k + P]
                            last = pe.transpose(t_bank[(NWU + k) % 2][:, rows * t:rows * t + rows], x_t, ident[0:rows, 0:rows])
                        last.then_inc(t_ready, 1)

                def step(ch, i, j, more):
                    i1, j1 = following(i, j)
                    k = 0
                    if more and out_proj:
                        project_out(ch + 1, i1, j1, unit(ch, 0), 0)
                        k = tiles
                    pe.wait_ge(t_free, ch * KT + NWU + KT + 2)
                    for q, (w, _, _, _, _) in enumerate(transposed):
                        for m in range(KT):
                            pe.wait_ge(out_free, unit(ch, k) + 1)
                            products(o_bank[k % OUT][:, 0:N], [(w_hi[w][:, q2, P * m:P * m + P], w_lo[w][:, q2, P * m:P * m + P],
                                                                hT_hi[:, j, q2, :], hT_lo[:, j, q2, :]) for q2 in range(KT)]).then_inc(out_ready, 1)
                            k += 1
                    if more and not router:
                        turn(ch + 1, i1, j1)
                    if v_out:
                        w = v_out[0]
                        for t in range(tiles):
                            pe.wait_ge(out_free, unit(ch, k) + 1)
                            cols = slice(rows * t, rows * t + rows)
                            products(o_bank[k % OUT][0:rows, :], [(hT_hi[:, j, q, cols], hT_lo[:, j, q, cols], w_hi[w][:, q, :], w_lo[w][:, q, :])
                                                                  for q in range(KT)]).then_inc(out_ready, 1)
                            k += 1
                    if router:
                        for t in range(tiles):
                            pe.wait_ge(out_free, unit(ch, k) + 1)
                            for q in range(KT):
                                last = pe.matmul(o_bank[k % OUT][0:rows, 0:8], hT_f[:, j, q, rows * t:rows * t + rows], wr_T[:, q, :],
                                                 start=(q == 0), stop=(q == KT - 1))
                            last.then_inc(out_ready, 1)
                            k += 1
                        if more:
                            turn(ch + 1, i1, j1)

                if out_proj:
                    pe.wait_ge(t_free, KT * (names.index(out_proj[0]) + 1) + 2)
                    project_out(0, 0, 0, 0, 0)
                turn(0, 0, 0)
                run(step)(pe)

            @block.scalar
            def _(act):
                for i, n in enumerate(names):
                    act.wait_ge(w_loaded[i], DMA)
                    for k in range(KT):
                        u = KT * i + k
                        act.wait_ge(t_ready, u + 1)
                        raw = t_bank[u % 2][:, :] if weights[n][1] == "oi" else w_raw[:, i % 2, k, :]
                        act.activation(w_hi[n][:, k, :], raw, ACT.Copy, scale=weights[n][2]).then_inc(hi_ready, 1)
                if router:
                    u = KT * len(names)
                    act.wait_ge(t_ready, u + 1)
                    act.activation(wr_T[:, :, :], t_bank[u % 2][:, 0:8 * KT].rearrange("p (k e) -> p k e", k=KT), ACT.Copy).then_inc(hi_ready, 1)
                act.wait_ge(bias_loaded, n_bias * DMA)
                for q, (_, _, s, _, _) in enumerate(transposed):
                    act.activation(b_col[:, q, :], b_raw[:, q, :], ACT.Copy, scale=s).then_inc(bias_ready, 1)
                if n_t:
                    act.wait_ge(bias_ready, n_t)

                def root(ch):
                    if stats_ln:
                        act.wait_ge(ve_done, ch + 1)
                        act.activation(std[:, :], veps[:, :], ACT.Sqrt).then_inc(std_done, 1)

                def turn(ch, j):
                    for k in range(KT):
                        act.wait_ge(t_ready, ch * KT + NWU + k + 1)
                        act.activation((hT_f if router else hT_hi)[:, j, k, :], t_bank[(NWU + k) % 2][:, 0:N], ACT.Copy).then_inc(hi_ready, 1)

                def step(ch, i, j, more):
                    if more:
                        root(ch + 1)
                    k = n_first if more else 0
                    if n_t:
                        act.wait_ge(stored[j], DMA + i * (n_stores * DMA))
                    for q in range(n_t):
                        for m in range(KT):
                            act.wait_ge(out_ready, unit(ch, k) + 1)
                            act.activation(t_hi[:, j, q, m, :], o_bank[k % OUT][:, 0:N], ACT.Identity,
                                           bias=b_col[:, q, m:m + 1]).then_inc(ohi_ready, 1)
                            k += 1
                    if more:
                        turn(ch + 1, 1 - j)

                root(0)
                turn(0, 0)
                run(step)(act)

            @block.vector
            def _(dve):
                dve.sem_inc(t_free, 2)
                dve.sem_inc(out_free, OUT)
                dve.sem_inc(x_done, AHEAD)
                dve.sem_inc(h_ready, AHEAD)
                for i, n in enumerate(names):
                    for k in range(KT):
                        u = KT * i + k
                        raw = t_bank[u % 2][:, :] if weights[n][1] == "oi" else w_raw[:, i % 2, k, :]
                        dve.wait_ge(hi_ready, u + 1)
                        dve.scalar_tensor_tensor(w_lo[n][:, k, :], raw, weights[n][2], as_f32(w_hi[n][:, k, :]),
                                                 ALU.mult, ALU.subtract).then_inc(t_free, 1)
                if router:
                    dve.wait_ge(hi_ready, KT * len(names) + 1)
                    dve.wait_ge(t_free, KT * len(names) + 2)
                    dve.sem_inc(t_free, 1)
                dve.wait_ge(bias_loaded, n_bias * DMA)
                if n_t:
                    dve.wait_ge(bias_ready, n_t)

                def residual(ch, i, j, u, k):
                    dve.wait_ge(x_stored[j], (i + 1) * DMA)
                    dve.wait_ge(x_loaded[j], (i + 1) * DMA)
                    for t in range(tiles):
                        dve.wait_ge(out_ready, u + k + t + 1)
                        dve.tensor_tensor(x_new[:, j, t, :], o_bank[(k + t) % OUT][0:rows, :], out_bias[0:rows, :], ALU.add).then_inc(out_free, 1)
                        dve.wait_ge(out_free, u + k + t + 1 + OUT)
                        dve.tensor_tensor(x_new[:, j, t, :], x_new[:, j, t, :], x_in[:, j, t, :], ALU.add).then_inc(x_done, 1)

                def normalise(ch, i, j):
                    x = x_new if out_proj else x_in
                    for t in range(tiles):
                        if out_proj:
                            dve.wait_ge(x_done, ch * tiles + t + 1 + AHEAD)
                        elif t == 0:
                            dve.wait_ge(x_loaded[j], (i + 1) * DMA)
                        dve.bn_stats(bn[:, t, :], x[:, j, t, :]).then_inc(bn_done, 1)
                    dve.wait_ge(bn_done, (ch + 1) * tiles)
                    dve.sem_inc(bn_seen, 1)
                    for t in range(tiles):
                        dve.bn_aggr(mv[:, t, :], bn[:, t, :]).then_inc(ag_done, 1)
                    dve.wait_ge(ag_done, (ch + 1) * tiles)
                    dve.tensor_scalar(veps[:, :], mv[:, :, 1], EPS, None, ALU.add).then_inc(ve_done, 1)
                    dve.wait_ge(std_done, ch + 1)
                    dve.reciprocal(rstd[:, :], std[:, :]).then_inc(rstd_done, 1)
                    dve.wait_ge(rstd_done, ch + 1)
                    dve.wait_ge(t_ready, ch * KT + NWU)
                    if router:
                        dve.wait_ge(h_stored, (ch + 1) * DMA)
                    for t in range(tiles):
                        dve.tensor_scalar(h[:, t, :], x[:, j, t, :], mv[:, t, 0:1], rstd[:, t:t + 1],
                                          ALU.subtract, ALU.mult).then_inc(h_ready, 1)

                def turn(ch, j):
                    for k in range(KT):
                        dve.wait_ge(hi_ready, ch * KT + NWU + k + 1)
                        if router:
                            dve.sem_inc(t_free, 1)
                        else:
                            dve.tensor_tensor(hT_lo[:, j, k, :], t_bank[(NWU + k) % 2][:, 0:N], as_f32(hT_hi[:, j, k, :]), ALU.subtract).then_inc(t_free, 1)

                def step(ch, i, j, more):
                    i1, j1 = following(i, j)
                    k = 0
                    if more and out_proj:
                        residual(ch + 1, i1, j1, unit(ch, 0), 0)
                        k = tiles
                    if more and stats_ln:
                        normalise(ch + 1, i1, j1)
                    for q in range(n_t):
                        for m in range(KT):
                            dve.wait_ge(ohi_ready, ch * (n_t * KT) + q * KT + m + 1)
                            dve.scalar_tensor_tensor(t_lo[:, j, q, m, :], o_bank[k % OUT][:, 0:N], b_col[:, q, m:m + 1], as_f32(t_hi[:, j, q, m, :]),
                                                     ALU.add, ALU.subtract).then_inc(out_free, 1)
                            k += 1
                    if more and not router:
                        turn(ch + 1, j1)
                    dve.wait_ge(stored[j], DMA + i * (n_stores * DMA))
                    for out, bias in ((v_out and v_sb, v_out and v_bias), (router and score, router and r_bias)):
                        for t in range(tiles if out else 0):
                            cols = slice(0, D if v_out else 8)
                            dve.wait_ge(out_ready, unit(ch, k) + 1)
                            dve.tensor_tensor(out[:, j, t, :], o_bank[k % OUT][0:rows, cols], bias[0:rows, :], ALU.add).then_inc(out_free, 1)
                            k += 1
                    if more and router:
                        turn(ch + 1, j1)

                if out_proj:
                    residual(0, 0, 0, 0, 0)
                if stats_ln:
                    normalise(0, 0, 0)
                turn(0, 0)
                run(step)(dve)


def constants(nc, sems, ident):
    cleared = sems.enter_context(nc.semaphore("const_cleared"))
    with nc.Block() as block:
        @block.gpsimd
        def _(pool):
            pool.memset(ident[:, :], 0.0).then_inc(cleared, 1)
            pool.wait_ge(cleared, 1)
            pool.affine_select(out=ident[:, :], in_=ident[:, :], compare_op=ALU.not_equal, fill=1.0,
                               base=0, pattern=[[-1, P]], channel_multiplier=1)


def attention_phase(nc, sems, tag, *, q, k, v, oT, keys, key_rows, ident, alibi):
    NK = keys // key_rows
    PAIRS = NK // 2
    LIN = (NK - 2) * key_rows
    FAR = keys - LIN
    assert not alibi or LIN <= SHIFT
    SU = PAIRS
    K1 = 104 if alibi else 96
    K2 = 104 if alibi else 100
    SLOTS = GROUPS if alibi else 2 * GROUPS
    ROUNDS = STEPS // SLOTS
    with Core(nc, sems) as c:
        q_st = c.sb(f"{tag}_q_st", [K2, SLOTS, 4, S], F32R)
        k_st = c.sb(f"{tag}_k_st", [K2, SLOTS, 4, keys], F32R)
        v_sb = c.sb(f"{tag}_v_sb", [key_rows, SLOTS, NK, P])
        ones = c.sb(f"{tag}_ones", [key_rows, DH])
        prob = c.sb(f"{tag}_prob", [key_rows, 2, 4, NK, S])
        k_const = c.sb(f"{tag}_k_const", [K2, keys])
        head_row = c.sb(f"{tag}_head_row", [K2, 4])
        part_max = c.sb(f"{tag}_part_max", [QR, 4, 2, 2])
        row_max = c.sb(f"{tag}_row_max", [QR, 2, 4])
        rinv = c.sb(f"{tag}_rinv", [P, S])
        o_f = c.sb(f"{tag}_o_f", [P, S])
        o_split = c.sb(f"{tag}_o_split", [P, 2, 2, S], F32R)
        if alibi:
            part_sum = c.sb(f"{tag}_part_sum", [key_rows, 2, 4, 2, S])
            rel_q = c.sb(f"{tag}_rel_q", [QR, 2, FAR], F32R)
            rel_k = c.sb(f"{tag}_rel_k", [key_rows, 2, S], F32R)
            rel_qf = c.sb(f"{tag}_rel_qf", [QR, 2, FAR])
            rel_kf = c.sb(f"{tag}_rel_kf", [key_rows, 2, S])
            q_grid = c.sb(f"{tag}_q_grid", [K2, S])
            q_lin = c.sb(f"{tag}_q_lin", [K2, 4, S])
            q_lin_hi = c.sb(f"{tag}_q_lin_hi", [K2, 4, S], F32R)
            is_lo = c.sb(f"{tag}_is_lo", [K2, 1])
            d_f = c.sb(f"{tag}_d_f", [P, 2, P])
            d_hi = c.sb(f"{tag}_d_hi", [P, HEADS, P], F32R)
            d_lo = c.sb(f"{tag}_d_lo", [P, HEADS // 2, P], F32R)
        SB, STB = (3, 3) if alibi else (2, 2)
        s_bank = [c.bank(f"{tag}_s_bank{i}") for i in range(SB)]
        st_bank = [c.bank(f"{tag}_st_bank{i}") for i in range(STB)]
        m_bank = st_bank[2] if alibi else c.bank(f"{tag}_m_bank")
        or_bank = [c.bank(f"{tag}_or_bank{i}") for i in range(2)]

        const_step = c.sem(f"{tag}_const_step")
        kconst_ready = c.sem(f"{tag}_kconst_ready")
        grid_ready = c.sem(f"{tag}_grid_ready")
        rel_ready = c.sem(f"{tag}_rel_ready")
        abs_ready = c.sem(f"{tag}_abs_ready")
        dstep = c.sem(f"{tag}_dstep")
        const_ready = c.sem(f"{tag}_const_ready")
        kstack_ready = c.sem(f"{tag}_kstack_ready")
        qstack_ready = c.sem(f"{tag}_qstack_ready")
        qk_loaded = [c.sem(f"{tag}_qk_loaded{i}") for i in range(SLOTS)]
        v_loaded = [c.sem(f"{tag}_v_loaded{i}") for i in range(SLOTS)]
        s_ready = c.sem(f"{tag}_s_ready")
        s_free = c.sem(f"{tag}_s_free")
        max_ready = c.sem(f"{tag}_max_ready")
        maxT_ready = c.sem(f"{tag}_maxT_ready")
        nm_ready = c.sem(f"{tag}_nm_ready")
        reset_done = c.sem(f"{tag}_reset_done")
        st_ready = c.sem(f"{tag}_st_ready")
        exp_done = c.sem(f"{tag}_exp_done")
        sum_done = c.sem(f"{tag}_sum_done")
        pv_done = c.sem(f"{tag}_pv_done")
        rinv_ready = c.sem(f"{tag}_rinv_ready")
        o_ready = c.sem(f"{tag}_o_ready")
        o_turn = c.sem(f"{tag}_o_turn")
        ohi_ready = c.sem(f"{tag}_ohi_ready")
        osplit_ready = c.sem(f"{tag}_osplit_ready")
        store_turn = c.sem(f"{tag}_store_turn")
        o_stored = [c.sem(f"{tag}_o_stored{i}") for i in range(2)]

        SPS, STS = 4 * SU, 4 * PAIRS

        def later(r, i, n):
            return r + (i + n) // SLOTS, (i + n) % SLOTS

        def batch_of(r, i):
            return r * (SLOTS // GROUPS) + i // GROUPS

        def run(engine, step, peeled=1):
            with engine.Fori(0, ROUNDS - peeled) as r:
                for i in range(SLOTS):
                    step(r * SLOTS + i, r, i, lambda n: True)
            for r in range(ROUNDS - peeled, ROUNDS):
                for i in range(SLOTS):
                    step(r * SLOTS + i, r, i, lambda n, s=r * SLOTS + i: s + n < STEPS)

        with nc.Block() as block:
            @block.gpsimd
            def _(pool):
                n = [0]

                def then(instruction):
                    n[0] += 1
                    instruction.then_inc(const_step, 1)
                    pool.wait_ge(const_step, n[0])

                if alibi:
                    grid = q_grid[96:K2, :]
                    then(pool.iota(grid, pattern=[[-1, S]], base=0, channel_multiplier=0, allow_small_or_imprecise_dtypes=True))
                    then(pool.affine_select(out=grid, in_=grid, compare_op=ALU.is_ge, fill=1.0, base=-6, pattern=[[0, S]], channel_multiplier=1))
                    then(pool.affine_select(out=grid, in_=grid, compare_op=ALU.is_ge, fill=0.0, base=-4, pattern=[[0, S]], channel_multiplier=1))
                    pool.sem_inc(grid_ready, 1)
                    lo = is_lo[96:K2, :]
                    then(pool.memset(lo, 0.0))
                    then(pool.affine_select(out=lo, in_=lo, compare_op=ALU.not_equal, fill=-1.0, base=-5, pattern=[[0, 1]], channel_multiplier=1))
                    then(pool.affine_select(out=lo, in_=lo, compare_op=ALU.not_equal, fill=-1.0, base=-7, pattern=[[0, 1]], channel_multiplier=1))
                    pool.sem_inc(grid_ready, 1)
                rows = head_row[96:K2, :]
                then(pool.memset(rows, 0.0))
                then(pool.affine_select(out=rows, in_=rows, compare_op=ALU.not_equal, fill=1.0, base=0, pattern=[[-1, 4]], channel_multiplier=1))
                kc = k_const[96:K2, :]
                if alibi:
                    then(pool.iota(kc, pattern=[[1, keys]], base=-SHIFT, channel_multiplier=0, allow_small_or_imprecise_dtypes=True))
                    then(pool.affine_select(out=kc, in_=kc, compare_op=ALU.is_ge, fill=1.0, base=5, pattern=[[0, keys]], channel_multiplier=-1))
                    then(pool.affine_select(out=kc, in_=kc, compare_op=ALU.is_ge, fill=0.0, base=LIN - 1, pattern=[[-1, keys]], channel_multiplier=0))
                    then(pool.affine_select(out=kc, in_=kc, compare_op=ALU.is_ge, fill=0.0, base=-4, pattern=[[0, keys]], channel_multiplier=1))
                else:
                    then(pool.memset(kc, 0.0))
                pool.sem_inc(kconst_ready, 1)
                if alibi:
                    grids = [(rel_qf[:, :, :], [[-QR, 2], [1, FAR]], LIN - SHIFT, -1),
                             (rel_kf[:, :, :], [[key_rows, 2], [-1, S]], LIN - SHIFT, 1)]
                    for grid, pattern, base, mult in grids:
                        then(pool.iota(grid, pattern=pattern, base=base, channel_multiplier=mult, allow_small_or_imprecise_dtypes=True))
                    pool.sem_inc(rel_ready, 1)
                then(pool.memset(ones[:, :], 1.0))
                pool.sem_inc(const_ready, 1)
                pool.sem_inc(osplit_ready, 1)
                pool.sem_inc(reset_done, SLOTS)

                def sums(s, i):
                    w = i % 2
                    pool.wait_ge(pv_done, s + 1)
                    for hh in range(4):
                        pool.wait_ge(exp_done, s * STS + hh * PAIRS + 2 + STB)
                        pool.tensor_tensor(part_sum[:, w, hh, :, :], prob[:, w, hh, 0:2, :], prob[:, w, hh, 2:4, :], ALU.add).then_inc(sum_done, 1)

                def reset(s, i):
                    pool.wait_ge(st_ready, (s + 1) * STS)
                    pool.wait_ge(sum_done, (s + 1) * 4)
                    pool.sem_inc(o_turn, 1)
                    pool.memset(as_f32(q_st[96:100, i, :, :]), 0.0).then_inc(reset_done, 1)
                    pool.wait_ge(reset_done, s + 1 + SLOTS)

                def split(s, r, i):
                    w = i % 2
                    pool.wait_ge(o_stored[w], (r * (SLOTS // 2) + i // 2 + 1) * DMA)
                    pool.wait_ge(o_ready, s + 3)
                    pool.sem_inc(o_turn, 1)
                    pool.tensor_copy(o_split[:, w, 0, :], o_f[:, :]).then_inc(ohi_ready, 1)
                    pool.wait_ge(ohi_ready, s + 1)
                    pool.tensor_tensor(o_split[:, w, 1, :], o_f[:, :], as_f32(o_split[:, w, 0, :]), ALU.subtract).then_inc(osplit_ready, 1)

                def weigh(s, i):
                    if alibi:
                        sums(s, i)
                        reset(s, i)

                def step(s, r, i, more):
                    if more(1):
                        weigh(s + 1, later(r, i, 1)[1])
                    split(s, r, i)

                weigh(0, 0)
                run(pool, step)

            @block.sync
            def _(sp):
                def load_qk(r, i):
                    b, g = batch_of(r, i), i % GROUPS
                    sp.dma_start(as_f32(q_st[0:96, i, :, :]), q[g, :, :, bass.ds(b * S, S)]).then_inc(qk_loaded[i], DMA)
                    sp.dma_start(as_f32(k_st[0:96, i, :, :]), k[g, :, :, bass.ds(b * keys, keys)]).then_inc(qk_loaded[i], DMA)

                def load_v(r, i):
                    b, g = batch_of(r, i), i % GROUPS
                    sp.dma_start(v_sb[:, i, :, :],
                                 v[bass.ds(b * keys, keys), P * g:P * g + P].rearrange("(t p) d -> p t d", p=key_rows)).then_inc(v_loaded[i], DMA)

                def reload_qk(s, r, i):
                    sp.wait_ge(st_ready, (s + 1) * STS)
                    sp.sem_inc(store_turn, 1)
                    load_qk(r + 1, i)

                def step(s, r, i, more):
                    b, g = batch_of(r, i), i % GROUPS
                    if more(SLOTS + 1):
                        reload_qk(s + 1, *later(r, i, 1))
                    if more(SLOTS):
                        sp.wait_ge(pv_done, s + 3)
                        sp.sem_inc(store_turn, 1)
                        load_v(r + 1, i)
                    sp.wait_ge(osplit_ready, s + 2)
                    sp.sem_inc(store_turn, 1)
                    sp.dma_start(oT[:, P * g:P * g + P, bass.ds(b * S, S)].rearrange("r p t -> p r t"),
                                 as_f32(o_split[:, i % 2, :, :])).then_inc(o_stored[i % 2], DMA)

                for i in range(SLOTS):
                    load_qk(0, i)
                    load_v(0, i)
                for w in range(2):
                    sp.sem_inc(o_stored[w], DMA)
                reload_qk(0, 0, 0)
                run(sp, step, peeled=2)
                for w in range(2):
                    sp.wait_ge(o_stored[w], (STEPS // 2 + 1) * DMA)

            @block.tensor
            def _(pe):
                def first_scores(s, r, i, hh, n):
                    hd = i % GROUPS * 4 + hh
                    if hh == 0 and n == 0:
                        pe.wait_ge(qk_loaded[i], (r + 1) * (2 * DMA))
                        if alibi:
                            pe.wait_ge(reset_done, s + 1)
                    far = alibi and n == 2
                    if far or not alibi:
                        units = [(t * (keys - LIN), t, LIN, keys) for t in range(2)]
                    else:
                        units = [(0, n, 0, LIN)]
                    bank = s_bank[(hh * SU + n) % SB]
                    pe.wait_ge(s_free, s * SPS + hh * SU + n + 1)
                    for col, t, k0, k1 in units:
                        last = pe.matmul(bank[0:QR, col:col + k1 - k0], q_st[0:K1, i, hh, QR * t:QR * t + QR], k_st[0:K1, i, hh, k0:k1],
                                         start=(col == 0), stop=not far, skip_group_check=True)
                    if far:
                        last = pe.matmul(bank[0:QR, 0:2 * FAR], d_hi[0:QR, hd, 0:QR], rel_q[:, :, :].rearrange("p t n -> p (t n)"),
                                         start=False, stop=True, skip_group_check=True)
                    last.then_inc(s_ready, 1)

                def second_scores(s, i, hh, u, more):
                    hd = i % GROUPS * 4 + hh
                    if hh == 0 and u == 0:
                        pe.wait_ge(nm_ready, s + 2)
                    n = hh * PAIRS + u
                    bank = st_bank[n % STB]
                    far = alibi and u == PAIRS - 1
                    pe.wait_ge(exp_done, s * STS + n + 1)
                    if bank is m_bank and n < STB and more:
                        pe.wait_ge(nm_ready, s + 3)
                    for e in range(2):
                        t = 2 * u + e
                        last = pe.matmul(bank[0:key_rows, S * e:S * e + S], k_st[:, i, hh, key_rows * t:key_rows * t + key_rows],
                                         q_st[:, i, hh, :], start=(e == 0), stop=not far, skip_group_check=True)
                    if far:
                        out, r = bank[0:key_rows, 0:2 * S], rel_k[:, :, :]
                        last = pe.matmul(out, d_hi[0:key_rows, hd, 0:key_rows], r, start=False, stop=(hd % 2 == 1), skip_group_check=True)
                        if hd % 2 == 0:
                            last = pe.matmul(out, d_lo[0:key_rows, hd // 2, 0:key_rows], r, start=False, stop=True, skip_group_check=True)
                    last.then_inc(st_ready, 1)

                def transpose_max(s, weights_before=True):
                    pe.wait_ge(max_ready, s + 1)
                    pe.wait_ge(nm_ready, s + 1)
                    if alibi and weights_before:
                        pe.wait_ge(exp_done, (s - 1) * STS + STB)
                    for t in range(2):
                        last = pe.transpose(m_bank[0:4, QR * t:QR * t + QR], row_max[:, t, :], ident[0:QR, 0:QR])
                    last.then_inc(maxT_ready, 1)

                def values(s, r, i, between):
                    w = i % 2
                    bank = or_bank[w]
                    pe.wait_ge(exp_done, (s + 1) * STS + STB)
                    pe.wait_ge(v_loaded[i], (r + 1) * DMA)
                    pe.wait_ge(o_ready, s + 1)
                    for t in range(NK):
                        for hh in range(4):
                            pe.matmul(bank[DH * hh:DH * hh + DH, 0:S], v_sb[:, i, t, DH * hh:DH * hh + DH], prob[:, w, hh, t, :],
                                      start=(t == 0), stop=(t == NK - 1), skip_group_check=True)
                    if alibi:
                        between()
                        pe.wait_ge(sum_done, (s + 1) * 4)
                        parts = [(prob, 4), (prob, 5), (part_sum, 0), (part_sum, 1)]
                    else:
                        parts = [(prob, 0), (prob, 1)]
                    for n, (weights, t) in enumerate(parts):
                        for hh in range(4):
                            last = pe.matmul(bank[DH * hh:DH * hh + DH, S:2 * S], ones[:, :], weights[:, w, hh, t, :],
                                             start=False, stop=(n == len(parts) - 1), skip_group_check=True)
                    last.then_inc(pv_done, 1)
                    if not alibi:
                        between()

                def scores(s, at, s2, at2, more=True):
                    for hh in range(4):
                        for n in range(PAIRS):
                            if at:
                                second_scores(s, at[1], hh, n, more)
                            if at2:
                                first_scores(s2, *at2, hh, n)

                def step(s, r, i, more):
                    scores(s + 1, more(1) and later(r, i, 1), s + 3, more(3) and later(r, i, 3), more(2))
                    values(s, r, i, lambda: more(3) and transpose_max(s + 3))

                pe.sem_inc(pv_done, 2)
                pe.sem_inc(maxT_ready, 1)
                for s in range(2):
                    pe.wait_ge(kstack_ready, s + 1)
                    if alibi:
                        pe.wait_ge(qstack_ready, s + 1)
                        pe.wait_ge(abs_ready, 2)
                    if s == 0:
                        pe.wait_ge(const_ready, 1)
                    scores(0, None, s, (0, s))
                    transpose_max(s, False)
                pe.wait_ge(kstack_ready, SLOTS)
                if alibi:
                    pe.wait_ge(qstack_ready, SLOTS)
                scores(0, (0, 0), 2, (0, 2))
                transpose_max(2)
                run(pe, step)

            @block.scalar
            def _(act):
                def minus_max(s, i):
                    act.wait_ge(maxT_ready, s + 2)
                    act.activation(q_st[96:100, i, :, :], m_bank[0:4, 0:S].unsqueeze(1).broadcast_to([4, 4, S]),
                                   ACT.Copy, scale=-1.0).then_inc(nm_ready, 1)

                def exps(s, i, middle):
                    act.wait_ge(pv_done, s + 1)
                    for n in range(STS):
                        if n == STS // 2 and not alibi:
                            middle()
                        act.wait_ge(st_ready, s * STS + n + 1)
                        hh, u = n // PAIRS, n % PAIRS
                        act.activation(prob[:, i % 2, hh, 2 * u:2 * u + 2, :], st_bank[n % STB][0:key_rows, 0:2 * S].rearrange("p (e q) -> p e q", e=2),
                                       ACT.Exp).then_inc(exp_done, 1)

                def step(s, r, i, more):
                    if more(1):
                        exps(s + 1, later(r, i, 1)[1], lambda: more(2) and minus_max(s + 2, later(r, i, 2)[1]))
                    if more(3) and alibi:
                        minus_max(s + 3, later(r, i, 3)[1])

                act.sem_inc(exp_done, STB)
                act.sem_inc(nm_ready, 1)
                act.wait_ge(kconst_ready, 1)
                for i in range(SLOTS):
                    for hh in range(4):
                        last = act.activation(k_st[96:K2, i, hh, :], k_const[96:K2, :], ACT.Identity, bias=head_row[96:K2, hh:hh + 1])
                    last.then_inc(kstack_ready, 1)
                    if alibi and i == 0:
                        act.wait_ge(rel_ready, 1)
                        act.activation(rel_q[:, :, :], rel_qf[:, :, :], ACT.Abs).then_inc(abs_ready, 1)
                        act.activation(rel_k[:, :, :], rel_kf[:, :, :], ACT.Abs).then_inc(abs_ready, 1)
                minus_max(0, 0)
                if alibi:
                    minus_max(1, 1)
                exps(0, 0, lambda: minus_max(1, 1))
                if alibi:
                    minus_max(2, 2)
                run(act, step)

            @block.vector
            def _(dve):
                def constants():
                    n = 0
                    dve.wait_ge(grid_ready, 2)
                    for g in range(GROUPS):
                        for hh in range(4):
                            last = dve.tensor_scalar(q_lin[96:K2, hh, :], q_grid[96:K2, :], slope(4 * g + hh), None, ALU.mult)
                        last.then_inc(dstep, 1)
                        dve.wait_ge(dstep, n + 1)
                        dve.tensor_copy(q_lin_hi[96:K2, :, :], q_lin[96:K2, :, :]).then_inc(dstep, 1)
                        for hd in range(4 * g, 4 * g + 4):
                            dve.tensor_scalar(d_hi[:, hd, :], ident[:, :], -slope(hd), None, ALU.mult).then_inc(dstep, 1)
                            if hd % 2 == 0:
                                dve.tensor_scalar(d_f[:, hd % 4 // 2, :], ident[:, :], -slope(hd), None, ALU.mult).then_inc(dstep, 1)
                        dve.wait_ge(dstep, n + 8)
                        dve.scalar_tensor_tensor(q_st[96:K2, g, :, :], as_f32(q_lin_hi[96:K2, :, :]), is_lo[96:K2, :], q_lin[96:K2, :, :],
                                                 ALU.mult, ALU.add).then_inc(dstep, 1)
                        for hd in range(4 * g, 4 * g + 4, 2):
                            dve.tensor_tensor(d_lo[:, hd // 2, :], d_f[:, hd % 4 // 2, :], as_f32(d_hi[:, hd, :]), ALU.subtract).then_inc(dstep, 1)
                        n += 11
                        dve.wait_ge(dstep, n)
                        dve.sem_inc(qstack_ready, 1)

                def maxima(s):
                    for n in range(SPS):
                        hh, u = n // SU, n % SU
                        dve.wait_ge(s_ready, s * SPS + n + 1)
                        bank = s_bank[n % SB][0:QR, :]
                        if not alibi:
                            if n == 0:
                                dve.wait_ge(maxT_ready, s + 1)
                            out, scores = row_max[:, :, hh], bank[:, 0:2 * keys].rearrange("p (t k) -> p t k", t=2)
                        elif u < 2:
                            out, scores = part_max[:, hh, u, 0:1], bank[:, 0:LIN]
                        else:
                            out, scores = part_max[:, hh, :, 1], bank[:, 0:2 * FAR].rearrange("p (t k) -> p t k", t=2)
                        dve.tensor_reduce(out, scores, AX.X, ALU.max).then_inc(s_free, 1)
                    dve.wait_ge(s_free, (s + 1) * SPS + SB)
                    if alibi:
                        dve.wait_ge(maxT_ready, s + 1)
                        dve.tensor_reduce(row_max[:, :, :].rearrange("p t h -> p h t"), part_max[:, :, :, :], AX.X, ALU.max).then_inc(max_ready, 1)
                    else:
                        dve.sem_inc(max_ready, 1)

                def normalise(s, i):
                    bank = or_bank[i % 2]
                    dve.wait_ge(o_ready, s + 2)
                    dve.wait_ge(pv_done, s + 3)
                    dve.reciprocal(rinv[:, :], bank[:, S:2 * S]).then_inc(rinv_ready, 1)
                    dve.wait_ge(rinv_ready, s + 1)
                    dve.wait_ge(osplit_ready, s + 1)
                    dve.tensor_tensor(o_f[:, :], bank[:, 0:S], rinv[:, :], ALU.mult).then_inc(o_ready, 1)

                def step(s, r, i, more):
                    if more(4):
                        maxima(s + 4)
                    normalise(s, i)

                dve.sem_inc(s_free, SB)
                dve.sem_inc(o_ready, 2)
                if alibi:
                    constants()
                for s in range(4):
                    maxima(s)
                run(dve, step)


EXPERTS, HID = 8, 1024
TILES = TOK // QR
STEP_ROWS = P
MOST_STEPS = -(-TOK // STEP_ROWS)
MOE_STEPS = -(-((2 * TOK + EXPERTS * (STEP_ROWS - 1)) // STEP_ROWS) // 2) * 2
PAIRS_AT = 2 * MOE_STEPS + 1
FETCHED = MOE_STEPS + 2
HCH = 4
HC = HID // HCH


class ExpertWeights:

    def __init__(self, c, w1, w2):
        self.w1, self.w2 = w1, w2
        self.w1_raw = c.sb("e_w1_raw", [P, HCH, KT, 2, HC])
        self.w2_raw = c.sb("e_w2_raw", [P, HCH, HC // P, D])
        self.w1_loaded = [c.sem(f"e_w1_loaded{i}") for i in range(HCH)]
        self.w2_loaded = [c.sem(f"e_w2_loaded{i}") for i in range(HCH)]

    def load_w1(self, sp, expert, q):
        for half in range(2):
            sp.dma_start(self.w1_raw[:, q, :, half, :], self.w1[bass.ds(expert, 1), :, HID * half + HC * q:HID * half + HC * q + HC]
                         .rearrange("o (k p) n -> p (o k) n", p=P)).then_inc(self.w1_loaded[q], DMA)

    def load_w2(self, sp, expert, q):
        sp.dma_start(self.w2_raw[:, q, :, :], self.w2[bass.ds(expert, 1), HC * q:HC * q + HC, :]
                     .rearrange("o (t p) d -> p (o t) d", p=P)).then_inc(self.w2_loaded[q], DMA)


def dispatch_phase(nc, sems, *, score, biases, token_of, slot_i, weight, step_table, expert_weights):
    TE = [QR, TILES, EXPERTS]
    with Core(nc, sems) as c:
        z = c.sb("d_z", TE)
        bias = c.sb("d_bias", [QR, EXPERTS])
        zb = c.sb("d_zb", TE)
        top = c.sb("d_top", TE)
        top_i = c.sb("d_top_i", TE, U32)
        top_f = c.sb("d_top_f", TE)
        iota_e = c.sb("d_iota_e", TE)
        pick = [c.sb(f"d_pick{j}", TE) for j in range(2)]
        mask = c.sb("d_mask", TE)
        before = c.sb("d_before", [QR, TILES + 1, EXPERTS])
        zmax = c.sb("d_zmax", [QR, TILES])
        zs = c.sb("d_zs", TE)
        e = c.sb("d_e", TE)
        esum = c.sb("d_esum", [QR, TILES])
        einv = c.sb("d_einv", [QR, TILES])
        w = c.sb("d_w", TE)
        prod = c.sb("d_prod", TE)
        val = [c.sb(f"d_val{j}", [QR, TILES]) for j in range(2)]
        vsum = c.sb("d_vsum", [QR, TILES])
        vinv = c.sb("d_vinv", [QR, TILES])
        earlier = c.sb("d_earlier", [QR, QR])
        ones = c.sb("d_ones", [QR, P])
        iota_m = c.sb("d_iota_m", [P, EXPERTS, MOST_STEPS])
        over = c.sb("d_over", [P, EXPERTS, MOST_STEPS])
        n_steps = c.sb("d_n_steps", [P, EXPERTS])
        begin = c.sb("d_begin", [P, EXPERTS + 1])
        first_row = c.sb("d_first_row", [P, EXPERTS])
        row = c.sb("d_row", TE)
        slot_f = c.sb("d_slot_f", [QR, 2, TILES])
        iota_s = c.sb("d_iota_s", [1, MOE_STEPS, EXPERTS])
        past = c.sb("d_past", [1, MOE_STEPS, EXPERTS])
        expert_f = c.sb("d_expert_f", [1, MOE_STEPS])
        expert_of = c.sb("d_expert_of", [1, MOE_STEPS])
        pairs_i = c.sb("d_pairs_i", [1, 1], I32)
        iota_lane = c.sb("d_iota_lane", [QR, STEP_ROWS])
        iota_step = c.sb("d_iota_step", [QR, FETCHED])
        token = c.sb("d_token", [QR, 2, TILES])
        slot_n = c.sb("d_slot_n", [QR, 2, TILES], I32)
        step_n = c.sb("d_step_n", [QR, 2, TILES], I32)
        step_f = c.sb("d_step_f", [QR, 2, TILES])
        step_row = c.sb("d_step_row", [QR, 2, TILES])
        lane_f = c.sb("d_lane_f", [QR, 2, TILES])
        at_lane = c.sb("d_at_lane", [QR, 2, TILES, STEP_ROWS], F32R)
        at_step = c.sb("d_at_step", [QR, 2, TILES, FETCHED])
        token_at_step = c.sb("d_token_at_step", [QR, 2, TILES, FETCHED], F32R)
        rank = c.bank("d_rank")
        total = c.bank("d_total")
        tokens = c.bank("d_tokens")
        loaded = c.sem("d_loaded")
        consts, consts2 = c.sem("d_consts"), c.sem("d_consts2")
        chain = c.sem("d_chain")
        exp_in, exp_out = c.sem("d_exp_in"), c.sem("d_exp_out")
        mask_ready, rank_ready = c.sem("d_mask_ready"), c.sem("d_rank_ready")
        places_ready, tokens_ready = c.sem("d_places_ready"), c.sem("d_tokens_ready")

        with nc.Block() as block:
            @block.sync
            def _(sp):
                sp.dma_start(z[:, :, :], score.rearrange("(t p) e -> p t e", p=QR)).then_inc(loaded, DMA)
                sp.dma_start(bias[:, :], biases.partition_broadcast(QR)).then_inc(loaded, DMA)
                for q in range(HCH):
                    expert_weights.load_w1(sp, 0, q)
                    expert_weights.load_w2(sp, 0, q)

            @block.gpsimd
            def _(pool):
                pool.memset(ones[:, :], 1.0).then_inc(consts, 1)
                pool.wait_ge(consts, 1)
                pool.memset(earlier[:, :], 1.0).then_inc(consts, 1)
                pool.wait_ge(consts, 2)
                pool.affine_select(out=earlier[:, :], in_=earlier[:, :], compare_op=ALU.is_gt, fill=0.0, base=0,
                                   pattern=[[1, QR]], channel_multiplier=-1).then_inc(consts, 1)
                pool.iota(iota_e[:, :, :], pattern=[[0, TILES], [1, EXPERTS]], base=0, channel_multiplier=0,
                          allow_small_or_imprecise_dtypes=True).then_inc(consts, 1)
                pool.iota(iota_m[:, :, :], pattern=[[0, EXPERTS], [STEP_ROWS, MOST_STEPS]], base=0, channel_multiplier=0,
                          allow_small_or_imprecise_dtypes=True).then_inc(consts, 1)
                pool.wait_ge(consts, 5)
                pool.iota(iota_s[:, :, :], pattern=[[1, MOE_STEPS], [0, EXPERTS]], base=0, channel_multiplier=0,
                          allow_small_or_imprecise_dtypes=True).then_inc(consts, 1)
                pool.iota(iota_lane[:, :], pattern=[[1, STEP_ROWS]], base=0, channel_multiplier=0,
                          allow_small_or_imprecise_dtypes=True).then_inc(consts2, 1)
                pool.iota(iota_step[:, :], pattern=[[1, FETCHED]], base=0, channel_multiplier=0,
                          allow_small_or_imprecise_dtypes=True).then_inc(consts2, 1)
                pool.iota(token[:, :, :], pattern=[[0, 2], [QR, TILES]], base=0, channel_multiplier=1,
                          allow_small_or_imprecise_dtypes=True).then_inc(consts2, 1)

            @block.tensor
            def _(pe):
                pe.wait_ge(consts, 6)
                pe.wait_ge(mask_ready, 1)
                te = lambda a: a.rearrange("p t e -> p (t e)")
                pe.matmul(rank[0:QR, 0:P], earlier[:, :], te(mask[:, :, :]), start=True, stop=False)
                pe.matmul(rank[0:QR, 0:P], ones[:, 0:QR], te(before[:, 0:TILES, :]), start=False, stop=True)
                pe.matmul(total[:, 0:EXPERTS], ones[:, :], before[:, TILES, :], start=True, stop=True).then_inc(rank_ready, 1)
                for j in range(2):
                    pe.wait_ge(places_ready, j + 1)
                    for t in range(TILES):
                        last = pe.matmul(tokens[:, 0:FETCHED], at_lane[:, j, t, :], token_at_step[:, j, t, :],
                                         start=(j == 0 and t == 0), stop=(j == 1 and t == TILES - 1))
                last.then_inc(tokens_ready, 1)

            @block.scalar
            def _(act):
                act.wait_ge(exp_in, 1)
                act.activation(e[:, :, :], zs[:, :, :], ACT.Exp).then_inc(exp_out, 1)

            @block.vector
            def _(dve):
                done = [0]

                def then(instruction):
                    done[0] += 1
                    instruction.then_inc(chain, 1)
                    dve.wait_ge(chain, done[0])

                def over_e(a):
                    return a.unsqueeze(2).broadcast_to(TE)

                def over_t(a):
                    return a.unsqueeze(1).broadcast_to(TE)

                dve.wait_ge(loaded, 2 * DMA)
                dve.wait_ge(consts, 6)
                then(dve.tensor_reduce(zmax[:, :], z[:, :, :], AX.X, ALU.max))
                dve.tensor_tensor(zs[:, :, :], z[:, :, :], over_e(zmax[:, :]), ALU.subtract).then_inc(exp_in, 1)
                then(dve.tensor_tensor(zb[:, :, :], z[:, :, :], over_t(bias[:, :]), ALU.add))
                for t in range(TILES):
                    last = dve.max(top[:, t, :], zb[:, t, :])
                then(last)
                for t in range(TILES):
                    last = dve.max_index(top_i[:, t, :], top[:, t, :], zb[:, t, :])
                then(last)
                then(dve.tensor_copy(top_f[:, :, :], top_i[:, :, :]))
                for j in range(2):
                    then(dve.tensor_tensor(pick[j][:, :, :], iota_e[:, :, :], over_e(top_f[:, :, j]), ALU.is_equal))
                then(dve.tensor_tensor(mask[:, :, :], pick[0][:, :, :], pick[1][:, :, :], ALU.add))
                then(dve.memset(before[:, 0, :], 0.0))
                for t in range(TILES):
                    then(dve.tensor_tensor(before[:, t + 1, :], before[:, t, :], mask[:, t, :], ALU.add))
                dve.sem_inc(mask_ready, 1)

                dve.wait_ge(exp_out, 1)
                then(dve.tensor_reduce(esum[:, :], e[:, :, :], AX.X, ALU.add))
                then(dve.reciprocal(einv[:, :], esum[:, :]))
                then(dve.tensor_tensor(w[:, :, :], e[:, :, :], over_e(einv[:, :]), ALU.mult))
                for j in range(2):
                    then(dve.tensor_tensor(prod[:, :, :], w[:, :, :], pick[j][:, :, :], ALU.mult))
                    then(dve.tensor_reduce(val[j][:, :], prod[:, :, :], AX.X, ALU.add))
                then(dve.tensor_tensor(vsum[:, :], val[0][:, :], val[1][:, :], ALU.add))
                then(dve.reciprocal(vinv[:, :], vsum[:, :]))
                for j in range(2):
                    then(dve.tensor_tensor(weight[:, j, :], val[j][:, :], vinv[:, :], ALU.mult))

                dve.wait_ge(rank_ready, 1)
                then(dve.tensor_tensor(over[:, :, :], total[:, 0:EXPERTS].unsqueeze(2).broadcast_to([P, EXPERTS, MOST_STEPS]), iota_m[:, :, :], ALU.is_gt))
                then(dve.tensor_reduce(n_steps[:, :], over[:, :, :], AX.X, ALU.add))
                then(dve.tensor_scalar(n_steps[:, 0:1], n_steps[:, 0:1], 1.0, None, ALU.max))
                then(dve.memset(begin[:, 0:1], 0.0))
                for x in range(EXPERTS):
                    then(dve.tensor_tensor(begin[:, x + 1:x + 2], begin[:, x:x + 1], n_steps[:, x:x + 1], ALU.add))
                then(dve.tensor_scalar(first_row[:, :], begin[:, 0:EXPERTS], float(STEP_ROWS), None, ALU.mult))
                then(dve.tensor_tensor(row[:, :, :], rank[0:QR, 0:P].rearrange("p (t e) -> p t e", e=EXPERTS),
                                       over_t(first_row[0:QR, :]), ALU.add))
                for j in range(2):
                    then(dve.tensor_tensor(prod[:, :, :], row[:, :, :], pick[j][:, :, :], ALU.mult))
                    then(dve.tensor_reduce(slot_f[:, j, :], prod[:, :, :], AX.X, ALU.add))
                dve.tensor_copy(slot_i[:, :, :], slot_f[:, :, :])
                dve.wait_ge(consts2, 3)
                then(dve.tensor_copy(slot_n[:, :, :], slot_f[:, :, :]))
                then(dve.tensor_scalar(step_n[:, :, :], slot_n[:, :, :], STEP_ROWS.bit_length() - 1, None, ALU.logical_shift_right))
                then(dve.tensor_copy(step_f[:, :, :], step_n[:, :, :]))
                then(dve.tensor_scalar(step_row[:, :, :], step_f[:, :, :], float(STEP_ROWS), None, ALU.mult))
                then(dve.tensor_tensor(lane_f[:, :, :], slot_f[:, :, :], step_row[:, :, :], ALU.subtract))
                LANES, STEPS_OF = [QR, TILES, STEP_ROWS], [QR, TILES, FETCHED]
                for j in range(2):
                    then(dve.tensor_tensor(at_step[:, j, :, :], iota_step[:, :].unsqueeze(1).broadcast_to(STEPS_OF),
                                           step_f[:, j, :].unsqueeze(2).broadcast_to(STEPS_OF), ALU.is_equal))
                    then(dve.tensor_tensor(token_at_step[:, j, :, :], at_step[:, j, :, :],
                                           token[:, j, :].unsqueeze(2).broadcast_to(STEPS_OF), ALU.mult))
                    dve.tensor_tensor(at_lane[:, j, :, :], iota_lane[:, :].unsqueeze(1).broadcast_to(LANES),
                                      lane_f[:, j, :].unsqueeze(2).broadcast_to(LANES), ALU.is_equal).then_inc(places_ready, 1)
                SE = [1, MOE_STEPS, EXPERTS]
                then(dve.tensor_tensor(past[:, :, :], iota_s[:, :, :], begin[0:1, 1:EXPERTS + 1].unsqueeze(1).broadcast_to(SE), ALU.is_ge))
                then(dve.tensor_reduce(expert_f[:, :], past[:, :, :], AX.X, ALU.add))
                then(dve.tensor_scalar(expert_of[:, :], expert_f[:, :], float(EXPERTS - 1), None, ALU.min))
                dve.tensor_copy(step_table[:, 0:MOE_STEPS], expert_of[:, :])
                dve.memset(step_table[:, MOE_STEPS:MOE_STEPS + 1], 1)
                then(dve.memset(step_table[:, 2 * MOE_STEPS:PAIRS_AT], 0))
                then(dve.tensor_tensor(step_table[:, MOE_STEPS + 1:2 * MOE_STEPS], expert_of[:, 1:MOE_STEPS], expert_of[:, 0:MOE_STEPS - 1], ALU.not_equal))
                then(dve.tensor_scalar(pairs_i[:, :], begin[0:1, EXPERTS:EXPERTS + 1], 1.0, None, ALU.add))
                then(dve.tensor_scalar(step_table[:, PAIRS_AT:PAIRS_AT + 1], pairs_i[:, :], 1, None, ALU.logical_shift_right))
                dve.wait_ge(tokens_ready, 1)
                then(dve.tensor_copy(token_of[:, :], tokens[:, 0:FETCHED]))


def expert_phase(nc, sems, *, h, token_of, out_rows, b1, b2, step_table, ident, expert_weights):
    HT = HC // P
    with Core(nc, sems) as c:
        x_in = c.sb("e_x_in", [P, 2, D])
        x_token = c.sb("e_x_token", [P, 2], U32)
        xT_hi = c.sb("e_xT_hi", [P, 2, KT, P], F32R)
        xT_lo = c.sb("e_xT_lo", [P, 2, KT, P], F32R)
        w1_raw, w2_raw = expert_weights.w1_raw, expert_weights.w2_raw
        w1_loaded, w2_loaded = expert_weights.w1_loaded, expert_weights.w2_loaded
        w1_hi = c.sb("e_w1_hi", [P, HCH, KT, 2, HC], F32R)
        w1_lo = c.sb("e_w1_lo", [P, HCH, KT, 2, HC], F32R)
        w2_hi = c.sb("e_w2_hi", [P, HCH, HT, D], F32R)
        w2_lo = c.sb("e_w2_lo", [P, HCH, HT, D], F32R)
        b1_row = c.sb("e_b1_row", [P, 2, 2, HID])
        b2_row = c.sb("e_b2_row", [P, 2, D])
        u_sb = c.sb("e_u_sb", [P, 2, 2, HC])
        gate = c.sb("e_gate", [P, 2, HC])
        g_sb = c.sb("e_g_sb", [P, 2, HC])
        g_hi = c.sb("e_g_hi", [P, 2, HT, P], F32R)
        g_lo = c.sb("e_g_lo", [P, 2, HT, P], F32R)
        y_sb = c.sb("e_y_sb", [P, 2, D])
        zeros = c.sb("e_zeros", [P, D])
        t_bank = [c.bank(f"e_t_bank{i}") for i in range(2)]
        u_bank = [c.bank(f"e_u_bank{i}") for i in range(2)]
        g_bank = [c.bank(f"e_g_bank{i}") for i in range(2)]
        y_bank = [c.bank(f"e_y_bank{i}") for i in range(2)]

        x_loaded = [c.sem(f"e_x_loaded{i}") for i in range(2)]
        b_loaded = [c.sem(f"e_b_loaded{i}") for i in range(2)]
        t_ready = c.sem("e_t_ready")
        xhi_ready = c.sem("e_xhi_ready")
        t_free = c.sem("e_t_free")
        w1hi_ready = c.sem("e_w1hi_ready")
        w1_ready = c.sem("e_w1_ready")
        w2hi_ready = c.sem("e_w2hi_ready")
        w2_ready = c.sem("e_w2_ready")
        up_ready = c.sem("e_up_ready")
        u_free = c.sem("e_u_free")
        gate_ready = c.sem("e_gate_ready")
        g_done = c.sem("e_g_done")
        gT_ready = c.sem("e_gT_ready")
        ghi_ready = c.sem("e_ghi_ready")
        glo_ready = c.sem("e_glo_ready")
        down_done = c.sem("e_down_done")
        y_ready = c.sem("e_y_ready")
        y_stored = [c.sem(f"e_y_stored{i}") for i in range(2)]
        slot_turn = c.sem("e_slot_turn")
        x_token_ready, fetch_turn = c.sem("e_x_token_ready"), c.sem("e_fetch_turn")
        zeros_ready = c.sem("e_zeros_ready")
        zeros_stored = c.sem("e_zeros_stored")

        def ahead(st, q, n):
            return (st + (q + n) // HCH, (q + n) % HCH)

        def use(i, j, n):
            return i + (j + n) // 2 + 1

        def rows_at(dram, step):
            return dram[bass.ds(step * STEP_ROWS, STEP_ROWS), :]

        def pairs_of(engine):
            return engine.value_load(step_table[0:1, PAIRS_AT:PAIRS_AT + 1], min_val=1, max_val=MOE_STEPS // 2)

        def is_other(engine, st):
            return engine.value_load(step_table[0:1, bass.ds(st + MOE_STEPS, 1)], min_val=0, max_val=1)

        def run(engine, step):
            pairs = pairs_of(engine)
            with engine.Fori(0, MOE_STEPS // 2) as i:
                with engine.If(i < pairs):
                    for j in range(2):
                        step(i * 2 + j, i, j)

        with nc.Block() as block:
            @block.sync
            def _(sp):
                def w1_slot(st, q):
                    sp.wait_ge(w1_ready, st * HCH + q + 1)
                    sp.sem_inc(slot_turn, 1)

                def w2_slot(st, q):
                    sp.wait_ge(w2_ready, st * HCH + q + 1)
                    sp.sem_inc(slot_turn, 1)

                def load(st, expert):
                    for q in range(HCH):
                        w1_slot(st, q)
                        expert_weights.load_w1(sp, expert, q)
                        w2_slot(st, q)
                        expert_weights.load_w2(sp, expert, q)

                def keep(st):
                    for q in range(HCH):
                        w1_slot(st, q)
                        sp.sem_inc(w1_loaded[q], 2 * DMA)
                        w2_slot(st, q)
                        sp.sem_inc(w2_loaded[q], DMA)

                def load_biases(st, expert, j):
                    sp.wait_ge(y_ready, st + 1)
                    sp.sem_inc(slot_turn, 1)
                    sp.dma_start(b1_row[:, j, :, :], b1[bass.ds(expert, 1), :].rearrange("o (h n) -> (o h) n", h=2).partition_broadcast(P)).then_inc(b_loaded[j], DMA)
                    sp.dma_start(b2_row[:, j, :], b2[bass.ds(expert, 1), :].rearrange("o d -> (o d)").partition_broadcast(P)).then_inc(b_loaded[j], DMA)

                def expert_of(st):
                    return sp.value_load(step_table[0:1, bass.ds(st, 1)], min_val=0, max_val=EXPERTS - 1)

                def step(st, j):
                    expert = expert_of(st + 1)
                    other = is_other(sp, st + 1)
                    with sp.If(other > 0):
                        load(st + 1, expert)
                    with sp.Else():
                        keep(st + 1)
                    load_biases(st + 1, expert, 1 - j)

                load_biases(0, 0, 0)
                pairs = pairs_of(sp)
                with sp.Fori(0, MOE_STEPS // 2) as i:
                    with sp.If(i < pairs):
                        for j in range(2):
                            step(i * 2 + j, j)
                sp.wait_ge(zeros_ready, 1)
                with sp.Fori(0, MOE_STEPS // 2) as i:
                    with sp.If(i < pairs):
                        sp.sem_inc(zeros_stored, 2 * DMA)
                    with sp.Else():
                        for j in range(2):
                            sp.dma_start(rows_at(out_rows, i * 2 + j), zeros[:, :]).then_inc(zeros_stored, DMA)
                for j in range(2):
                    sp.wait_ge(y_stored[j], (pairs + 1) * DMA)
                    sp.sem_inc(slot_turn, 1)
                sp.wait_ge(zeros_stored, MOE_STEPS * DMA)

            @block.tensor
            def _(pe):
                def turn(st, slot, uses):
                    pe.wait_ge(x_loaded[slot], uses * DMA)
                    pe.wait_ge(t_free, st + 1)
                    for k in range(KT):
                        last = pe.transpose(t_bank[slot][:, P * k:P * k + P], x_in[:, slot, P * k:P * k + P], ident[:, :])
                    last.then_inc(t_ready, 1)

                def up(st, q, slot):
                    pe.wait_ge(w1_ready, st * HCH + q + HCH + 1)
                    pe.wait_ge(u_free, st * HCH + q + 1)
                    if q == 0:
                        pe.wait_ge(t_free, st + 3)
                    out = u_bank[q % 2][:, :]
                    for k in range(KT):
                        w_h, w_l = (w[:, q, k, :, :].rearrange("p h n -> p (h n)") for w in (w1_hi, w1_lo))
                        pe.matmul(out, xT_hi[:, slot, k, :], w_h, start=(k == 0), stop=False)
                        pe.matmul(out, xT_hi[:, slot, k, :], w_l, start=False, stop=False)
                        last = pe.matmul(out, xT_lo[:, slot, k, :], w_h, start=False, stop=(k == KT - 1))
                    last.then_inc(up_ready, 1)

                def turn_gated(st, q):
                    pe.wait_ge(g_done, st * HCH + q + 3)
                    pe.wait_ge(glo_ready, st * HCH + q + 1)
                    for t in range(HT):
                        last = pe.transpose(g_bank[q % 2][:, P * t:P * t + P], g_sb[:, q % 2, P * t:P * t + P], ident[:, :])
                    last.then_inc(gT_ready, 1)

                def down(st, q, slot):
                    pe.wait_ge(w2_ready, st * HCH + q + HCH + 1)
                    pe.wait_ge(glo_ready, st * HCH + q + 3)
                    if q == 0:
                        pe.wait_ge(y_ready, st + 1)
                    for t in range(HT):
                        first, end = q == 0 and t == 0, q == HCH - 1 and t == HT - 1
                        pe.matmul(y_bank[slot][:, :], g_hi[:, q % 2, t, :], w2_hi[:, q, t, :], start=first, stop=False)
                        pe.matmul(y_bank[slot][:, :], g_hi[:, q % 2, t, :], w2_lo[:, q, t, :], start=False, stop=False)
                        last = pe.matmul(y_bank[slot][:, :], g_lo[:, q % 2, t, :], w2_hi[:, q, t, :], start=False, stop=end)
                    last.then_inc(down_done, 1)

                def step(st, i, j):
                    turn(st + 1, 1 - j, use(i, j, 1))
                    for q in range(HCH):
                        n = (q + 2) // HCH
                        up(*ahead(st, q, 2), (j + n) % 2)
                        turn_gated(*ahead(st, q, 1))
                        down(st, q, j)

                pe.sem_inc(t_ready, 1)
                pe.sem_inc(up_ready, HCH)
                pe.sem_inc(down_done, HCH)
                pe.sem_inc(gT_ready, 2)
                turn(0, 0, 1)
                up(0, 0, 0)
                up(0, 1, 0)
                turn_gated(0, 0)
                run(pe, step)

            @block.scalar
            def _(act):
                def turn(st, slot):
                    act.wait_ge(t_ready, st + 2)
                    act.activation(xT_hi[:, slot, :, :], t_bank[slot][:, :].rearrange("p (k n) -> p k n", k=KT), ACT.Copy).then_inc(xhi_ready, 1)

                def silu(st, q):
                    act.wait_ge(g_done, st * HCH + q + 1)
                    act.wait_ge(u_free, st * HCH + q + 3)
                    act.activation(gate[:, q % 2, :], u_sb[:, q % 2, 0, :], ACT.Silu).then_inc(gate_ready, 1)

                def gated_hi(st, q):
                    act.wait_ge(gT_ready, st * HCH + q + 3)
                    act.wait_ge(down_done, st * HCH + q + HCH - 1)
                    act.activation(g_hi[:, q % 2, :, :], g_bank[q % 2][:, 0:HC].rearrange("p (t n) -> p t n", t=HT), ACT.Copy).then_inc(ghi_ready, 1)

                def split_w1(st, q):
                    act.wait_ge(w1_loaded[q], (st + 1) * (2 * DMA))
                    act.wait_ge(up_ready, st * HCH + q + 1)
                    act.activation(w1_hi[:, q, :, :, :], w1_raw[:, q, :, :, :], ACT.Copy).then_inc(w1hi_ready, 1)

                def split_w2(st, q):
                    act.wait_ge(w2_loaded[q], (st + 1) * DMA)
                    act.wait_ge(down_done, st * HCH + q + 1)
                    act.activation(w2_hi[:, q, :, :], w2_raw[:, q, :, :], ACT.Copy).then_inc(w2hi_ready, 1)

                def pass_on(ready, st, q):
                    act.wait_ge(ready, st * HCH + q)
                    act.sem_inc(ready, 1)

                def step(st, i, j):
                    other = is_other(act, st + 1)
                    for q in range(HCH):
                        gated_hi(*ahead(st, q, 1))
                        with act.If(other > 0):
                            split_w1(st + 1, q)
                            silu(*ahead(st, q, 2))
                            if q:
                                split_w2(st + 1, q - 1)
                            if q == HCH - 1:
                                split_w2(st + 1, q)
                        with act.Else():
                            pass_on(w1hi_ready, st + 1, q)
                            silu(*ahead(st, q, 2))
                            if q:
                                pass_on(w2hi_ready, st + 1, q - 1)
                            if q == HCH - 1:
                                pass_on(w2hi_ready, st + 1, q)
                        if q == 0:
                            turn(st + 1, 1 - j)
                    act.wait_ge(y_ready, st + 3)
                    act.dma_start(rows_at(out_rows, st), y_sb[:, j, :]).then_inc(y_stored[j], DMA)

                act.sem_inc(y_stored[0], DMA)
                act.sem_inc(y_stored[1], DMA)
                for q in range(HCH):
                    split_w1(0, q)
                    if q == HCH - 2:
                        turn(0, 0)
                split_w2(0, 0)
                silu(0, 0)
                gated_hi(0, 0)
                silu(0, 1)
                for q in range(1, HCH):
                    split_w2(0, q)
                run(act, step)

            @block.gpsimd
            def _(pool):
                def split_w2(st, q):
                    pool.wait_ge(w2hi_ready, st * HCH + q + 1)
                    pool.tensor_tensor(w2_lo[:, q, :, :], w2_raw[:, q, :, :], as_f32(w2_hi[:, q, :, :]),
                                       ALU.subtract).then_inc(w2_ready, 1)

                def fetch(st, slot):
                    pool.tensor_copy(x_token[:, slot:slot + 1], token_of[:, bass.ds(st, 1)]).then_inc(x_token_ready, 1)
                    pool.wait_ge(x_token_ready, st + 1)
                    pool.sem_inc(fetch_turn, 1)
                    pool.indirect_dma_start(x_in[:, slot, :], None, h,
                                            bass.IndirectOffsetOnAxis(ap=x_token[:, slot:slot + 1], axis=0)).then_inc(x_loaded[slot], DMA)

                def step(st, i, j):
                    pool.wait_ge(t_ready, st + 2)
                    pool.sem_inc(fetch_turn, 1)
                    fetch(st + 2, j)
                    other = is_other(pool, st + 1)
                    with pool.If(other > 0):
                        for q in range(HCH):
                            split_w2(st + 1, q)
                    with pool.Else():
                        for q in range(HCH):
                            pool.wait_ge(w2hi_ready, (st + 1) * HCH + q + 1)
                            pool.wait_ge(w2_ready, (st + 1) * HCH + q + HCH)
                            pool.sem_inc(w2_ready, 1)

                fetch(0, 0)
                fetch(1, 1)
                pool.memset(zeros[:, :], 0.0).then_inc(zeros_ready, 1)
                pool.wait_ge(zeros_ready, 1)
                pool.sem_inc(w2_ready, HCH)
                for q in range(HCH):
                    split_w2(0, q)
                run(pool, step)
                pairs = pairs_of(pool)
                for j in range(2):
                    pool.wait_ge(x_loaded[j], (pairs + 1) * DMA)
                    pool.sem_inc(fetch_turn, 1)

            @block.vector
            def _(dve):
                def turn(st, slot):
                    dve.wait_ge(xhi_ready, st + 1)
                    dve.tensor_tensor(xT_lo[:, slot, :, :], t_bank[slot][:, :].rearrange("p (k n) -> p k n", k=KT),
                                      as_f32(xT_hi[:, slot, :, :]), ALU.subtract).then_inc(t_free, 1)

                def split_w1(st, q):
                    dve.wait_ge(w1hi_ready, st * HCH + q + 1)
                    dve.tensor_tensor(w1_lo[:, q, :, :, :], w1_raw[:, q, :, :, :], as_f32(w1_hi[:, q, :, :, :]),
                                      ALU.subtract).then_inc(w1_ready, 1)

                def add_bias(st, q, slot, uses):
                    if q == 0:
                        dve.wait_ge(b_loaded[slot], uses * (2 * DMA))
                    dve.wait_ge(up_ready, st * HCH + q + HCH + 1)
                    dve.tensor_tensor(u_sb[:, q % 2, :, :], u_bank[q % 2][:, :].rearrange("p (h n) -> p h n", h=2),
                                      b1_row[:, slot, :, HC * q:HC * q + HC], ALU.add).then_inc(u_free, 1)

                def multiply(st, q):
                    dve.wait_ge(gate_ready, st * HCH + q + 1)
                    dve.wait_ge(gT_ready, st * HCH + q + 1)
                    dve.tensor_tensor(g_sb[:, q % 2, :], gate[:, q % 2, :], u_sb[:, q % 2, 1, :], ALU.mult).then_inc(g_done, 1)

                def gated_lo(st, q):
                    dve.wait_ge(ghi_ready, st * HCH + q + 1)
                    dve.tensor_tensor(g_lo[:, q % 2, :, :], g_bank[q % 2][:, 0:HC].rearrange("p (t n) -> p t n", t=HT),
                                      as_f32(g_hi[:, q % 2, :, :]), ALU.subtract).then_inc(glo_ready, 1)

                def step(st, i, j):
                    other = is_other(dve, st + 1)
                    for q in range(HCH):
                        n = (q + 2) // HCH
                        add_bias(*ahead(st, q, 2), (j + n) % 2, use(i, j, n))
                        gated_lo(*ahead(st, q, 1))
                        multiply(*ahead(st, q, 2))
                        with dve.If(other > 0):
                            split_w1(st + 1, q)
                        with dve.Else():
                            dve.wait_ge(w1hi_ready, (st + 1) * HCH + q + 1)
                            dve.wait_ge(w1_ready, (st + 1) * HCH + q + HCH)
                            dve.sem_inc(w1_ready, 1)
                        if q == 0:
                            turn(st + 1, 1 - j)
                    dve.wait_ge(down_done, (st + 2) * HCH)
                    dve.wait_ge(y_stored[j], (i + 1) * DMA)
                    dve.tensor_tensor(y_sb[:, j, :], y_bank[j][:, :], b2_row[:, j, :], ALU.add).then_inc(y_ready, 1)

                dve.sem_inc(t_free, 2)
                dve.sem_inc(w1_ready, HCH)
                dve.sem_inc(u_free, 2)
                dve.sem_inc(g_done, 2)
                dve.sem_inc(glo_ready, 2)
                dve.sem_inc(y_ready, 2)
                for q in range(HCH):
                    split_w1(0, q)
                    if q == 1:
                        turn(0, 0)
                add_bias(0, 0, 0, 1)
                multiply(0, 0)
                gated_lo(0, 0)
                add_bias(0, 1, 0, 1)
                multiply(0, 1)
                run(dve, step)


def combine_phase(nc, sems, *, x, out_rows, slot_i, weight, out):
    with Core(nc, sems) as c:
        x_sb = c.sb("c_x", [QR, TILES, D])
        y = [c.sb(f"c_y{j}", [QR, TILES, D]) for j in range(2)]
        x_loaded = c.sem("c_x_loaded")
        gathered = [c.sem(f"c_gathered{t}") for t in range(TILES)]
        added = [c.sem(f"c_added{j}") for j in range(2)]
        stored = c.sem("c_stored")
        tiles = "(t p) d -> p t d"
        with nc.Block() as block:
            @block.sync
            def _(sp):
                sp.dma_start(x_sb[:, :, :], x.rearrange(tiles, p=QR)).then_inc(x_loaded, DMA)
                for t in range(0, TILES, 2):
                    sp.wait_ge(added[1], t + 2)
                    sp.dma_start(out.rearrange(tiles, p=QR)[:, t:t + 2, :], x_sb[:, t:t + 2, :]).then_inc(stored, DMA)
                sp.wait_ge(stored, TILES // 2 * DMA)

            @block.gpsimd
            def _(pool):
                for t in range(TILES):
                    for j in range(2):
                        pool.indirect_dma_start(y[j][:, t, :], None, out_rows,
                                                bass.IndirectOffsetOnAxis(ap=slot_i[:, j, t:t + 1], axis=0)).then_inc(gathered[t], DMA)

            @block.vector
            def _(dve):
                dve.wait_ge(x_loaded, DMA)
                for t in range(TILES):
                    dve.wait_ge(gathered[t], 2 * DMA)
                    for j in range(2):
                        if j:
                            dve.wait_ge(added[0], t + 1)
                        dve.scalar_tensor_tensor(x_sb[:, t, :], y[j][:, t, :], weight[:, j, t:t + 1], x_sb[:, t, :],
                                                 ALU.mult, ALU.add).then_inc(added[j], 1)


INPUTS = ["x", "ctx_1024"] + ["L0_attn_" + n for n in ("q_w", "q_b", "k_w", "k_b", "v_w", "v_b", "out_w", "out_b")] + \
         ["L0_xattn_" + n for n in ("Wq", "bq", "Wkv", "bkv", "Wo", "bo")] + \
         ["L0_ffn_" + n for n in ("Wr", "br", "Wl1", "bl1", "Wl2", "bl2", "biases_N")]


def build(nc, d, out):
    def scratch(name, shape):
        return nc.dram_tensor(name, shape, F32, kind="Internal").ap()

    flat = "b s d -> (b s) d"
    x, ctx = d["x"].rearrange(flat), d["ctx_1024"].rearrange(flat)
    q1, k1, q2 = (scratch(n, [GROUPS, 3 * DH, 4, TOK]) for n in ("q1", "k1", "q2"))
    k2, v2 = scratch("k2", [GROUPS, 3 * DH, 4, B * CTX]), scratch("v2", [B * CTX, D])
    oT1, oT2 = (scratch(n, [2, D, TOK]) for n in ("oT1", "oT2"))
    v1, x1, x2, h = (scratch(n, [TOK, D]) for n in ("v1", "x1", "x2", "h_moe"))
    score = scratch("score", [TOK, EXPERTS])
    out_rows = scratch("out_rows", [MOE_STEPS * STEP_ROWS, D])
    a, c, f = "L0_attn_", "L0_xattn_", "L0_ffn_"
    token_tiles = dict(rows=QR, tiles=4, chunks=TOK // QR // 4)

    with ExitStack() as sems:
        ident = sems.enter_context(nc.sbuf_tensor("ident", [P, P], F32))
        slot_i = sems.enter_context(nc.sbuf_tensor("slot_i", [QR, 2, TILES], U32))
        weight = sems.enter_context(nc.sbuf_tensor("weight", [QR, 2, TILES], F32))
        step_table = sems.enter_context(nc.sbuf_tensor("step_table", [1, PAIRS_AT + 1], I32))
        constants(nc, sems, ident)
        linear_phase(nc, sems, "p1", src=x, ident=ident, **token_tiles, stats_ln=True,
                     weights={"wq": (d[a + "q_w"], "oi", QSCALE), "wk": (d[a + "k_w"], "oi", 1.0), "wv": (d[a + "v_w"], "oi", 1.0)},
                     transposed=[("wq", d[a + "q_b"], QSCALE, q1, QUERY_PARTS), ("wk", d[a + "k_b"], 1.0, k1, KEY_PARTS)],
                     v_out=("wv", d[a + "v_b"], v1))
        linear_phase(nc, sems, "p2", src=ctx, ident=ident, rows=CR, tiles=4, chunks=B * CTX // CR // 4, stats_ln=False,
                     weights={"wk": (d[c + "Wkv"][:, 0:D], "io", 1.0), "wv": (d[c + "Wkv"][:, D:2 * D], "io", 1.0)},
                     transposed=[("wk", d[c + "bkv"][0:D], 1.0, k2, KEY_PARTS)], v_out=("wv", d[c + "bkv"][D:2 * D], v2))
        attention_phase(nc, sems, "a1", q=q1, k=k1, v=v1, oT=oT1, keys=S, key_rows=QR, ident=ident, alibi=False)
        linear_phase(nc, sems, "o1", src=None, ident=ident, **token_tiles, stats_ln=True,
                     weights={"wo": (d[a + "out_w"], "oi", 1.0), "wq": (d[c + "Wq"], "io", QSCALE)},
                     out_proj=("wo", d[a + "out_b"], oT1, x, x1),
                     transposed=[("wq", d[c + "bq"], QSCALE, q2, QUERY_PARTS)])
        attention_phase(nc, sems, "a2", q=q2, k=k2, v=v2, oT=oT2, keys=CTX, key_rows=CR, ident=ident, alibi=True)
        linear_phase(nc, sems, "o2", src=None, ident=ident, **token_tiles, stats_ln=True,
                     weights={"wo": (d[c + "Wo"], "io", 1.0)},
                     out_proj=("wo", d[c + "bo"], oT2, x1, x2), transposed=[],
                     router=(d[f + "Wr"], d[f + "br"], score, h))
        token_of = sems.enter_context(nc.sbuf_tensor("token_of", [P, FETCHED], F32))
        with Core(nc, sems) as both:
            expert_weights = ExpertWeights(both, d[f + "Wl1"], d[f + "Wl2"])
            dispatch_phase(nc, sems, score=score, biases=d[f + "biases_N"], token_of=token_of,
                           slot_i=slot_i, weight=weight, step_table=step_table, expert_weights=expert_weights)
            expert_phase(nc, sems, h=h, token_of=token_of, out_rows=out_rows, b1=d[f + "bl1"], b2=d[f + "bl2"],
                         step_table=step_table, ident=ident, expert_weights=expert_weights)
        combine_phase(nc, sems, x=x2, out_rows=out_rows, slot_i=slot_i, weight=weight, out=out.rearrange(flat))


def kernel(**inputs):
    import concourse.bacc as bacc
    from concourse.bass_utils import run_bass_kernel_spmd

    nc = bacc.Bacc("TRN2", target_bir_lowering=False, num_devices=1)
    arrays = {n: np.ascontiguousarray(inputs[n]) for n in INPUTS}
    d = {n: nc.dram_tensor(n, a.shape, F32, kind="ExternalInput").ap() for n, a in arrays.items()}
    out = nc.dram_tensor("out", (B, S, D), F32, kind="ExternalOutput").ap()
    build(nc, d, out)
    return run_bass_kernel_spmd(nc, [arrays], core_ids=[0]).results[0]["out"]
```
